# Optimizing a Trainium2 kernel written in Bass

```python
import numpy as np
import jax
import jax.numpy as jnp

def _softmax(x, axis=-1):
    return jax.nn.softmax(x, axis=axis)

def _gelu(x):
    return jax.nn.gelu(x, approximate=True)

def _silu(x):
    return jax.nn.silu(x)

def _sigmoid(x):
    return jax.nn.sigmoid(x)

def _layernorm(x, axis=-1, eps=1e-05):
    m = jnp.mean(x, axis=axis, keepdims=True)
    v = jnp.var(x, axis=axis, keepdims=True)
    return (x - m) / jnp.sqrt(v + eps)

def _scatter_add(tgt, idx, src, axis=0):
    return tgt.at[idx].add(src)

def _segment_sum(src, seg, n):
    return jax.ops.segment_sum(src, seg, n)
kernel_name = 'mk_sandwich_d1_jaxref_r8_49f40a'

def setup_inputs(seed: int=0):
    np.random.seed(seed)
    _w = jnp.asarray

    def _L0_attn_setup():
        import jax, jax.numpy as jnp
        import numpy as np
        HEADS = 8
        DIM_HEAD = 128
        BLOCK_N = 128

        def castle_attention(q, k, v, qu, ku, vu, scale):
            b, h, s, d = q.shape
            q = q * scale
            qu = qu * scale
            qk = jnp.einsum('bhid,bhjd->bhij', q, k)
            quku = jnp.einsum('bhid,bhjd->bhij', qu, ku)
            i = jnp.arange(s)[:, None]
            j = jnp.arange(s)[None, :]
            causal = i >= j
            qk = jnp.where(causal, qk, -jnp.inf)
            la = jnp.where(causal, 0.0, jax.nn.sigmoid(quku))
            nb = s // BLOCK_N
            la_b = la.reshape(b, h, s, nb, BLOCK_N)
            vu_b = vu.reshape(b, h, nb, BLOCK_N, d)
            su = jnp.einsum('bhmtc,bhtcd->bhmtd', la_b, vu_b)
            scores = qk.reshape(b, h, s, nb, BLOCK_N) - jax.nn.silu(su)
            scores = scores.reshape(b, h, s, s)
            p = jax.nn.softmax(scores, axis=-1)
            return jnp.einsum('bhij,bhjd->bhid', p, v)
        key = jax.random.key(seed)
        k1, k2, k3 = jax.random.split(key, 3)
        B, S, D = (1, 256, 128)
        dim_inner = HEADS * DIM_HEAD
        x = jax.random.normal(k1, (B, S, D), dtype=jnp.float32)
        w_qkv = jax.random.normal(k2, (D, 6 * dim_inner), dtype=jnp.float32) * 0.02
        w_out = jax.random.normal(k3, (dim_inner, D), dtype=jnp.float32) * 0.02
        return {'x': x, 'w_qkv': w_qkv, 'w_out': w_out}
    _L0_attn_in = _L0_attn_setup()

    def _L0_ffn_setup():
        import jax, jax.numpy as jnp
        import numpy as np
        B, L, D = (2, 256, 128)
        E = 15
        H = D * 1
        K = 3
        T = 1.0
        key = jax.random.key(seed)
        ks = jax.random.split(key, 12)
        s = 0.02
        return {'x': jax.random.normal(ks[0], (B, L, D), dtype=jnp.float32), 'router_W': jax.random.normal(ks[1], (D, E), dtype=jnp.float32) * s, 'router_b': jnp.zeros((E,), dtype=jnp.float32), 'sW1': jax.random.normal(ks[2], (D, H), dtype=jnp.float32) * s, 'sb1': jnp.zeros((H,), dtype=jnp.float32), 'sW2': jax.random.normal(ks[3], (H, D), dtype=jnp.float32) * s, 'sb2': jnp.zeros((D,), dtype=jnp.float32), 'eW1': jax.random.normal(ks[4], (E, D, H), dtype=jnp.float32) * s, 'eb1': jnp.zeros((E, H), dtype=jnp.float32), 'eW2': jax.random.normal(ks[5], (E, H, D), dtype=jnp.float32) * s, 'eb2': jnp.zeros((E, D), dtype=jnp.float32)}
    _L0_ffn_in = _L0_ffn_setup()
    _d = {'L0_attn_x': _L0_attn_in['x'], 'L0_attn_w_qkv': _L0_attn_in['w_qkv'], 'L0_attn_w_out': _L0_attn_in['w_out'], 'L0_ffn_router_W': _L0_ffn_in['router_W'], 'L0_ffn_router_b': _L0_ffn_in['router_b'], 'L0_ffn_sW1': _L0_ffn_in['sW1'], 'L0_ffn_sb1': _L0_ffn_in['sb1'], 'L0_ffn_sW2': _L0_ffn_in['sW2'], 'L0_ffn_sb2': _L0_ffn_in['sb2'], 'L0_ffn_eW1': _L0_ffn_in['eW1'], 'L0_ffn_eb1': _L0_ffn_in['eb1'], 'L0_ffn_eW2': _L0_ffn_in['eW2'], 'L0_ffn_eb2': _L0_ffn_in['eb2']}
    _x0 = _d['L0_attn_x']
    _d['L0_attn_x'] = jax.random.normal(jax.random.fold_in(jax.random.key(seed), 1), (8, 512, 128), dtype=_x0.dtype)
    del _x0
    return _d

def reference(L0_attn_x, L0_attn_w_qkv, L0_attn_w_out, L0_ffn_router_W, L0_ffn_router_b, L0_ffn_sW1, L0_ffn_sb1, L0_ffn_sW2, L0_ffn_sb2, L0_ffn_eW1, L0_ffn_eb1, L0_ffn_eW2, L0_ffn_eb2):

    def _L0_attn_ref(x, w_qkv, w_out):
        import jax, jax.numpy as jnp
        import numpy as np
        HEADS = 8
        DIM_HEAD = 128
        BLOCK_N = 128

        def castle_attention(q, k, v, qu, ku, vu, scale):
            b, h, s, d = q.shape
            q = q * scale
            qu = qu * scale
            qk = jnp.einsum('bhid,bhjd->bhij', q, k)
            quku = jnp.einsum('bhid,bhjd->bhij', qu, ku)
            i = jnp.arange(s)[:, None]
            j = jnp.arange(s)[None, :]
            causal = i >= j
            qk = jnp.where(causal, qk, -jnp.inf)
            la = jnp.where(causal, 0.0, jax.nn.sigmoid(quku))
            nb = s // BLOCK_N
            la_b = la.reshape(b, h, s, nb, BLOCK_N)
            vu_b = vu.reshape(b, h, nb, BLOCK_N, d)
            su = jnp.einsum('bhmtc,bhtcd->bhmtd', la_b, vu_b)
            scores = qk.reshape(b, h, s, nb, BLOCK_N) - jax.nn.silu(su)
            scores = scores.reshape(b, h, s, s)
            p = jax.nn.softmax(scores, axis=-1)
            return jnp.einsum('bhij,bhjd->bhid', p, v)
        B, S, D = x.shape
        scale = DIM_HEAD ** (-0.5)
        qkvs = (x @ w_qkv).reshape(B, S, 6, HEADS, DIM_HEAD)
        qkvs = jnp.transpose(qkvs, (2, 0, 3, 1, 4))
        qu, ku, vu, qc, kc, vc = (qkvs[t] for t in range(6))
        o = castle_attention(qc, kc, vc, qu, ku, vu, scale)
        o = jnp.transpose(o, (0, 2, 1, 3)).reshape(B, S, HEADS * DIM_HEAD)
        return o @ w_out

    def _L0_ffn_ref(x, router_W, router_b, sW1, sb1, sW2, sb2, eW1, eb1, eW2, eb2):
        import jax, jax.numpy as jnp
        import numpy as np
        B, L, D = (2, 256, 128)
        E = 15
        H = D * 1
        K = 3
        T = 1.0
        b, l, d = x.shape
        n = b * l
        xt = x.reshape(n, d)
        shared = jax.nn.relu(xt @ sW1 + sb1) @ sW2 + sb2
        logits = xt @ router_W + router_b
        probs = jax.nn.softmax(logits / T, axis=-1)
        top_p, top_i = jax.lax.top_k(probs, K)
        cw = jnp.zeros((n, E), dtype=probs.dtype)
        cw = cw.at[jnp.arange(n)[:, None], top_i].set(top_p)
        h = jax.nn.relu(jnp.einsum('nd,edh->neh', xt, eW1) + eb1)
        ye = jnp.einsum('neh,ehd->ned', h, eW2) + eb2
        routed = jnp.einsum('ned,ne->nd', ye, cw)
        return (shared + routed).reshape(b, l, d)
    x = L0_attn_x
    x = x + _layernorm(_L0_attn_ref(_layernorm(x, axis=-1), L0_attn_w_qkv, L0_attn_w_out), axis=-1)
    x = x + _layernorm(_L0_ffn_ref(_layernorm(x, axis=-1), L0_ffn_router_W, L0_ffn_router_b, L0_ffn_sW1, L0_ffn_sb1, L0_ffn_sW2, L0_ffn_sb2, L0_ffn_eW1, L0_ffn_eb1, L0_ffn_eW2, L0_ffn_eb2), axis=-1)
    return x

_drawn_inputs = setup_inputs


def setup_inputs(seed=0):
    import zlib

    import numpy as np

    out = dict(_drawn_inputs(seed))
    spreads = {'L0_ffn_router_b': (0.0, 0.1),
     'L0_ffn_sb1': (0.0, 0.1),
     'L0_ffn_sb2': (0.0, 0.1),
     'L0_ffn_eb1': (0.0, 0.669),
     'L0_ffn_eb2': (0.0, 0.1)}
    factors = {}
    for name, (base, spread) in spreads.items():
        noise = np.random.default_rng([zlib.crc32(name.encode()), seed]).standard_normal(out[name].shape)
        drawn = base * np.exp(spread * noise) if base else spread * noise
        out[name] = jnp.asarray(drawn.astype(out[name].dtype))
    for name, factor in factors.items():
        out[name] = (out[name] * factor).astype(out[name].dtype)
    return out
```

```python
import concourse.bass as bass
from concourse import mybir
from contextlib import ExitStack

P = 128
B, S, D = 8, 512, 128
H = 8
NT = S // P
E = 15
EA = E + 1
TOPK = 3
ROUTE_STEPS = 8
SCALE = float(D) ** -0.5
EPS = 1e-5
MASKED = -1e30
BIG = 3e38
F32 = mybir.dt.float32
F32R = mybir.dt.float32r
ROWS = [3, 2, 1, 0]
QKVS = dict(qu=0, ku=1, vu=2, q=3, k=4, v=5)


def castle_moe(nc, x, w_qkv, w_out, router_w, router_b, s_w1, s_b1, s_w2, s_b2, e_w1, e_b1, e_w2, e_b2, out):
    ALU, ACT, AX = mybir.AluOpType, mybir.ActivationFunctionType, mybir.AxisListType
    ctx = ExitStack()
    with ctx:
        def sb(name, shape, dt=F32):
            return ctx.enter_context(nc.sbuf_tensor(name, shape, dt))

        def sem(name):
            return ctx.enter_context(nc.semaphore(name))

        values = sb("values", [P, 2, NT, H * D])
        vu, vp = values[:, 0], values[:, 1]
        w_raw = values[:, :, :, :].rearrange("p a t n -> p (a t n)")[:, 0:6 * H * D]
        work = sb("work", [P, 8192])
        w_t = work[:, 0:5 * 1024].rearrange("p (m n) -> p m n", m=5)
        w1_raw = work[:, 5 * 1024:7 * 1024].rearrange("p (e n) -> p e n", e=EA)
        probs = work[:, 0:2048].rearrange("p (i j) -> p i j", i=NT)
        neg_silu = work[:, 2048:4096].rearrange("p (i j) -> p i j", i=NT)
        diag = work[:, 2048:2048 + NT * (S + P)].rearrange("p (i j) -> p i j", j=S + P)[:, :, 0:P]
        probs_t = [work[:, 4096 + 2048 * n:6144 + 2048 * n].rearrange("p (j i) -> p j i", j=NT) for n in range(2)]
        wo_raw = sb("wo_raw", [P, H, D])
        mq_hi, mq_lo = sb("mq_hi", [P, H * D], F32R), sb("mq_lo", [P, H * D], F32R)
        mu_hi, mu_lo = sb("mu_hi", [P, H * D], F32R), sb("mu_lo", [P, H * D], F32R)
        wv_hi, wv_lo = sb("wv_hi", [P, H * D], F32R), sb("wv_lo", [P, H * D], F32R)
        wu_hi, wu_lo = sb("wu_hi", [P, H * D], F32R), sb("wu_lo", [P, H * D], F32R)
        w1_hi, w1_lo = sb("w1_hi", [P, EA, D], F32R), sb("w1_lo", [P, EA, D], F32R)
        w2 = sb("w2", [P, EA, D])
        b1_raw, b1 = sb("b1_raw", [EA, D]), sb("b1", [P, EA])
        b2 = sb("b2", [EA, D])
        rw, rb, ones_row = sb("rw", [P, E]), sb("rb", [1, E]), sb("ones_row", [1, P])
        ident, quarter = sb("ident", [P, P]), sb("quarter", [P, NT, P])
        lower = sb("lower", [P, E, E])
        half_power = sb("half_power", [P, NT])
        x_in, x_res = sb("x_in", [P, NT, D]), sb("x_res", [P, NT, D])
        xn = sb("xn", [P, NT, D])
        xn_t, xn_hi, xn_lo = sb("xn_t", [P, S]), sb("xn_hi", [P, S], F32R), sb("xn_lo", [P, S], F32R)
        q_hi, q_lo, qu_t = sb("q_hi", [P, S], F32R), sb("q_lo", [P, S], F32R), sb("qu_t", [P, S])
        la_t, tanh_su = sb("la_t", [P, NT, P]), sb("tanh_su", [P, NT, P])
        neg_max, row_sum, row_inv = sb("neg_max", [P, NT]), sb("row_sum", [P, NT]), sb("row_inv", [P, NT])
        att_t = sb("att_t", [P, S])
        stats, mv = sb("stats", [P, NT, 6]), sb("mv", [P, NT, 2])
        var_eps, rstd = sb("var_eps", [P, NT]), sb("rstd", [P, NT])
        normed, x1, x1n = sb("normed", [P, NT, D]), sb("x1", [P, NT, D]), sb("x1n", [P, NT, D])
        y_t, y_hi, y_lo = sb("y_t", [P, S]), sb("y_hi", [P, S], F32R), sb("y_lo", [P, S], F32R)
        top, route_sum, route_inv = sb("top", [P, NT]), sb("route_sum", [P, NT]), sb("route_inv", [P, NT])
        logits, gates = sb("logits", [P, NT, E]), sb("gates", [P, NT, E])
        above, tied, rank = sb("above", [P, NT, E, E]), sb("tied", [P, NT, E, E]), sb("rank", [P, NT, E])
        cw, cw_t = sb("cw", [P, NT, EA]), sb("cw_t", [EA, S])
        hidden = [sb(f"hidden{n}", [P, S]) for n in range(2)]
        ffn, result = sb("ffn", [P, NT, D]), sb("result", [P, NT, D])

        bank = [ctx.enter_context(nc.psum_tensor(f"bank{n}", [P, 512], F32)) for n in range(8)]
        b_att, b_q, b_u, b_la = bank[0], bank[1], bank[2], bank[3]
        b_rows, b_pt = bank[4:6], bank[6:8]

        names = """w_loaded x_loaded ffn_loaded res_loaded consts_made stored
            wt_made wt_moved_a wt_moved_v prod_made prod_hi prod_lo wu_hi_made w1_hi_made splits_made b1_made b1_moved
            xn_ready xt_made xt_moved xhi_made xlo_made x1_ready val_made val_moved_a val_moved_v
            q_made u_made qhi_made qlo_made u_moved quku_made tanh_la la_made su_made tanh_made silu_made silu_masked
            row_made row_maxed row_exped inv_made row_normed pt_made pt_moved att_made att_moved atok_made
            stats_made mv_made var_ready rstd_ready x1n_ready normed_made yt_made yt_moved yhi_made ylo_made
            logits_made logits_shifted gates_exped route_step cw_ready cwt_made cwt_moved bias_made ffn_init
            hid_made hid_ready ye_made ye_added result_ready""".split()
        s = {n: sem(n) for n in names}

        block = ctx.enter_context(nc.Block())
        xv = x.rearrange("b (t p) d -> b p t d", p=P)
        ov = out.rearrange("b (t p) d -> b p t d", p=P)
        order = ["qu", "ku", "q", "k", "v"]
        products = [("mu", 0, 1), ("mq", 2, 3), ("wv", 4, None)]
        prod_dst = dict(mu=(mu_hi, mu_lo), mq=(mq_hi, mq_lo), wv=(wv_hi, wv_lo))

        @block.sync
        def _(sp):
            sp.dma_start(x_in[:, :, :], xv[0]).then_inc(s["x_loaded"], 16)
            for n in range(6):
                sp.dma_start(w_raw[:, n * 1024:(n + 1) * 1024], w_qkv[:, n * 1024:(n + 1) * 1024]).then_inc(s["w_loaded"], 16)
            sp.dma_start(wo_raw[:, :, :], w_out.rearrange("(h p) n -> p h n", p=P)).then_inc(s["w_loaded"], 16)
            sp.dma_start(w1_raw[:, 0:E, :], e_w1.rearrange("e d n -> d e n")).then_inc(s["ffn_loaded"], 16)
            sp.dma_start(w1_raw[:, E, :], s_w1).then_inc(s["ffn_loaded"], 16)
            sp.dma_start(w2[:, 0:E, :], e_w2.rearrange("e d n -> d e n")).then_inc(s["ffn_loaded"], 16)
            sp.dma_start(w2[:, E, :], s_w2).then_inc(s["ffn_loaded"], 16)
            sp.dma_start(b1_raw[0:E, :], e_b1).then_inc(s["ffn_loaded"], 16)
            sp.dma_start(b1_raw[E:EA, :], s_b1.rearrange("(a n) -> a n", a=1)).then_inc(s["ffn_loaded"], 16)
            sp.dma_start(b2[0:E, :], e_b2).then_inc(s["ffn_loaded"], 16)
            sp.dma_start(b2[E:EA, :], s_b2.rearrange("(a n) -> a n", a=1)).then_inc(s["ffn_loaded"], 16)
            sp.dma_start(rw[:, :], router_w).then_inc(s["ffn_loaded"], 16)
            sp.dma_start(rb[:, :], router_b.rearrange("(a n) -> a n", a=1)).then_inc(s["stored"], 16)

            def batch(b, after, b_res):
                sp.wait_ge(s["xn_ready"], b + 1)
                sp.dma_start(x_in[:, :, :], xv[after]).then_inc(s["x_loaded"], 16)
                if b_res is not None:
                    sp.wait_ge(s["x1_ready"], b_res)
                sp.dma_start(x_res[:, :, :], xv[b]).then_inc(s["res_loaded"], 16)
                sp.wait_ge(s["result_ready"], b + 1)
                sp.dma_start(ov[b], result[:, :, :]).then_inc(s["stored"], 16)

            batch(0, 1, None)
            with sp.Fori(1, B - 1) as b:
                batch(b, b + 1, b)
            batch(B - 1, B - 1, B - 1)
            sp.wait_ge(s["stored"], 16 * (B + 1))

        @block.gpsimd
        def _(pool):
            g = nc.gpsimd
            silu_count, row_count = pool.alloc_register("silu_count"), pool.alloc_register("row_count")
            pool.reg_mov(silu_count, 0)
            pool.reg_mov(row_count, 0)
            g.memset(ident[:, :], 0.0).then_inc(s["consts_made"], 1)
            g.memset(quarter[:, :, :], 0.25).then_inc(s["consts_made"], 1)
            g.memset(lower[:, :, :], 1.0).then_inc(s["consts_made"], 1)
            g.memset(half_power[:, :], -0.5).then_inc(s["consts_made"], 1)
            g.memset(ones_row[:, :], 1.0).then_inc(s["consts_made"], 1)
            g.memset(cw[:, :, E:EA], 1.0).then_inc(s["consts_made"], 1)
            pool.wait_ge(s["consts_made"], 6)
            g.affine_select(out=ident[:, :], in_=ident[:, :], compare_op=ALU.not_equal, fill=1.0, base=0,
                            pattern=[[-1, P]], channel_multiplier=1).then_inc(s["consts_made"], 1)
            g.affine_select(out=quarter[:, :, :], in_=quarter[:, :, :], compare_op=ALU.is_gt, fill=0.0, base=0,
                            pattern=[[0, NT], [-1, P]], channel_multiplier=1).then_inc(s["consts_made"], 1)
            g.affine_select(out=lower[:, :, :], in_=lower[:, :, :], compare_op=ALU.is_gt, fill=0.0, base=0,
                            pattern=[[1, E], [-1, E]], channel_multiplier=0).then_inc(s["consts_made"], 1)

            def inv_sqrt(n):
                pool.wait_ge(s["var_ready"], n)
                g.tensor_tensor(rstd[:, :], var_eps[:, :], half_power[:, :], ALU.pow).then_inc(s["rstd_ready"], 1)

            def mask_silu():
                pool.reg_add(silu_count, silu_count, 1)
                pool.wait_ge(s["consts_made"], 9)
                pool.wait_ge(s["silu_made"], silu_count)
                g.affine_select(out=diag, in_=diag, compare_op=ALU.is_ge, fill=MASKED, base=0,
                                pattern=[[0, NT], [-1, P]], channel_multiplier=1).then_inc(s["silu_masked"], 1)

            inv_sqrt(1)
            mask_silu()
            with pool.Fori(0, B) as b:
                for h in range(H):
                    for n, i in enumerate(ROWS):
                        pool.reg_add(row_count, row_count, 1)
                        pool.wait_ge(s["consts_made"], 9)
                        pool.wait_ge(s["inv_made"], row_count)
                        w = (i + 1) * P
                        g.tensor_scalar(probs[:, i, 0:w], probs[:, i, 0:w], row_inv[:, i:i + 1], 1.0,
                                        ALU.mult, ALU.mult).then_inc(s["row_normed"], 1)
                    if h == 2:
                        inv_sqrt(4 * b + 2)
                    if h < H - 1:
                        mask_silu()
                inv_sqrt(4 * b + 3)
                inv_sqrt(4 * b + 4)
                mask_silu()
                inv_sqrt(4 * b + 5)

        @block.tensor
        def _(pe):
            mm = nc.tensor.matmul

            def mm3(dst, a_hi, a_lo, c_hi, c_lo, start=True, stop=True):
                mm(dst, a_lo, c_hi, start=start, stop=False)
                mm(dst, a_hi, c_lo, start=False, stop=False)
                return mm(dst, a_hi, c_hi, start=False, stop=stop)

            def tile(t):
                return slice(t * P, (t + 1) * P)

            def transpose_x():
                for t in range(NT):
                    last = nc.tensor.transpose(b_q[:, tile(t)], xn[:, t, :], ident[:, :])
                last.then_inc(s["xt_made"], 1)

            def value_group(k, first, moved_a, moved_v):
                dst = (b_u, b_la)[k % 2]
                if not first:
                    pe.wait_ge(s["val_moved_a" if k % 2 == 0 else "val_moved_v"], (moved_a, moved_v)[k % 2])
                hi, lo = ((wu_hi, wu_lo), (wv_hi, wv_lo))[k // 8]
                t, half = (k % 8) // 2, k % 2
                c = slice(half * 512, half * 512 + 512)
                mm3(dst[:, :], xn_hi[:, tile(t)], xn_lo[:, tile(t)], hi[:, c], lo[:, c]).then_inc(s["val_made"], 1)

            def project_u(h):
                c = slice(h * D, (h + 1) * D)
                mm3(b_u[:, :], mu_hi[:, c], mu_lo[:, c], xn_hi[:, :], xn_lo[:, :]).then_inc(s["u_made"], 1)

            def project_q(h):
                c = slice(h * D, (h + 1) * D)
                mm3(b_q[:, :], mq_hi[:, c], mq_lo[:, c], xn_hi[:, :], xn_lo[:, :]).then_inc(s["q_made"], 1)

            def lookahead_logits(g1):
                pe.wait_ge(s["u_moved"], g1)
                for t in range(NT):
                    last = mm(b_la[:, tile(t)], xn_t[:, tile(t)], qu_t[:, tile(t)], start=True, stop=True)
                last.then_inc(s["quku_made"], 1)

            def lookahead_sum(h, g1):
                pe.wait_ge(s["la_made"], g1)
                for t in range(NT):
                    last = mm(b_la[:, tile(t)], la_t[:, t, :], vu[:, t, h * D:(h + 1) * D], start=True, stop=True)
                last.then_inc(s["su_made"], 1)

            def score_row(n):
                i = ROWS[n]
                w = (i + 1) * P
                mm3(b_rows[n % 2][:, 0:w], q_hi[:, tile(i)], q_lo[:, tile(i)], xn_hi[:, 0:w], xn_lo[:, 0:w])\
                    .then_inc(s["row_made"], 1)

            def transpose_rows(rows, dst, signal=True):
                at = 0
                for i in rows:
                    for j in range(i + 1):
                        last = nc.tensor.transpose(dst[:, at:at + P], probs[:, i, tile(j)], ident[:, :])
                        at += P
                last.then_inc(s["pt_made"], 1)

            def attend(h, j):
                return mm(b_att[:, j * P:S], vp[:, j, h * D:(h + 1) * D], probs_t[h % 2][:, j, j * P:S],
                          start=(h == 0 and j == 0), stop=(h == H - 1 and j == NT - 1), skip_group_check=True)

            def hidden_layer(e):
                mm3(b_rows[e % 2][:, :], w1_hi[:, e, :], w1_lo[:, e, :], y_hi[:, :], y_lo[:, :]).then_inc(s["hid_made"], 1)

            def output_layer(b, e):
                pe.wait_ge(s["hid_ready"], EA * b + e + 1)
                if e >= 2:
                    pe.wait_ge(s["ye_added"], EA * b + e - 1)
                for t in range(NT):
                    last = mm(b_pt[e % 2][:, tile(t)], hidden[e % 2][:, tile(t)], w2[:, e, :], start=True, stop=True)
                last.then_inc(s["ye_made"], 1)

            pe.wait_ge(s["consts_made"], 9)
            for k in range(10):
                m, half = k // 2, k % 2
                if k == 0:
                    pe.wait_ge(s["w_loaded"], 16 * 7)
                if k >= 4:
                    pe.wait_ge(s["wt_moved_a" if k % 2 == 0 else "wt_moved_v"], (k - 4) // 2 + 1)
                for n in range(4):
                    h = half * 4 + n
                    c = QKVS[order[m]] * 1024 + h * D
                    last = nc.tensor.transpose(bank[k % 4][:, tile(n)], w_raw[:, c:c + D], ident[:, :])
                last.then_inc(s["wt_made"], 1)
            pe.wait_ge(s["wt_moved_a"], 5)
            pe.wait_ge(s["wt_moved_v"], 5)
            k = 0
            for name, left, right in products:
                for half in range(2):
                    for n in range(4):
                        h = half * 4 + n
                        rhs = wo_raw[:, h, :] if right is None else w_t[:, right, h * D:(h + 1) * D]
                        last = mm(bank[k][:, tile(n)], w_t[:, left, h * D:(h + 1) * D], rhs, start=True, stop=True)
                    last.then_inc(s["prod_made"], 1)
                    k += 1
            pe.wait_ge(s["ffn_loaded"], 16 * 9)
            nc.tensor.transpose(bank[6][:, 0:EA], b1_raw[:, :], ident[0:EA, 0:EA]).then_inc(s["b1_made"], 1)

            pe.wait_ge(s["xn_ready"], 1)
            pe.wait_ge(s["prod_lo"], 6)
            transpose_x()
            pe.wait_ge(s["xlo_made"], 1)
            pe.wait_ge(s["xt_moved"], 1)
            pe.wait_ge(s["splits_made"], 1)
            for k in range(16):
                value_group(k, k < 2, k // 2, k // 2)
            pe.wait_ge(s["val_moved_a"], 8)
            pe.wait_ge(s["val_moved_v"], 8)
            project_u(0)
            project_q(0)
            lookahead_logits(1)
            lookahead_sum(0, 1)

            with pe.Fori(0, B) as b:
                for h in range(H):
                    g0 = H * b + h
                    pe.wait_ge(s["qhi_made"], g0 + 1)
                    pe.wait_ge(s["qlo_made"], g0 + 1)
                    score_row(0)
                    score_row(1)
                    if h:
                        pe.wait_ge(s["pt_moved"], 3 * g0)
                        attend(h - 1, 0)
                    pe.wait_ge(s["row_maxed"], 4 * g0 + 1)
                    score_row(2)
                    pe.wait_ge(s["row_maxed"], 4 * g0 + 2)
                    score_row(3)
                    if h:
                        attend(h - 1, 1)
                    if h < H - 1:
                        project_u(h + 1)
                        project_q(h + 1)
                        lookahead_logits(g0 + 2)
                    pe.wait_ge(s["row_normed"], 4 * g0 + 1)
                    transpose_rows([3], b_pt[0])
                    pe.wait_ge(s["row_normed"], 4 * g0 + 4)
                    transpose_rows([2, 0], b_pt[1])
                    pe.wait_ge(s["pt_moved"], 3 * g0 + 1)
                    transpose_rows([1], b_pt[0])
                    if h:
                        attend(h - 1, 2)
                        attend(h - 1, 3)
                    if h < H - 1:
                        lookahead_sum(h + 1, g0 + 2)
                pe.wait_ge(s["xn_ready"], b + 2)
                transpose_x()
                pe.wait_ge(s["xlo_made"], b + 2)
                pe.wait_ge(s["xt_moved"], b + 2)
                for k in range(2):
                    value_group(k, True, 0, 0)
                pe.wait_ge(s["pt_moved"], 3 * (H * b + H))
                for j in range(NT):
                    last = attend(H - 1, j)
                last.then_inc(s["att_made"], 1)
                for k in range(2, 8):
                    value_group(k, False, 8 * b + 8 + k // 2, 8 * b + 8 + k // 2)
                pe.wait_ge(s["att_moved"], b + 1)
                for t in range(NT):
                    last = nc.tensor.transpose(b_pt[0][:, tile(t)], att_t[:, tile(t)], ident[:, :])
                last.then_inc(s["atok_made"], 1)
                for k in range(8, 16):
                    value_group(k, False, 8 * b + 8 + k // 2, 8 * b + 8 + k // 2)
                pe.wait_ge(s["val_moved_a"], 8 * b + 16)
                pe.wait_ge(s["val_moved_v"], 8 * b + 16)
                pe.wait_ge(s["x1n_ready"], b + 1)
                for t in range(NT):
                    last = nc.tensor.transpose(b_pt[1][:, tile(t)], x1n[:, t, :], ident[:, :])
                last.then_inc(s["yt_made"], 1)
                project_u(0)
                project_q(0)
                pe.wait_ge(s["yt_moved"], b + 1)
                for t in range(NT):
                    c = slice(t * 16, t * 16 + E)
                    mm(b_pt[0][:, c], y_t[:, tile(t)], rw[:, :], start=True, stop=False)
                    last = mm(b_pt[0][:, c], ones_row[:, :], rb[:, :], start=False, stop=True)
                last.then_inc(s["logits_made"], 1)
                lookahead_logits(H * b + H + 1)
                pe.wait_ge(s["ylo_made"], b + 1)
                hidden_layer(0)
                hidden_layer(1)
                lookahead_sum(0, H * b + H + 1)
                pe.wait_ge(s["cw_ready"], b + 1)
                for t in range(NT):
                    last = nc.tensor.transpose(b_pt[0][0:EA, tile(t)], cw[:, t, :], ident[:, :])
                last.then_inc(s["cwt_made"], 1)
                pe.wait_ge(s["cwt_moved"], b + 1)
                for t in range(NT):
                    last = mm(b_pt[1][:, tile(t)], cw_t[:, tile(t)], b2[:, :], start=True, stop=True)
                last.then_inc(s["bias_made"], 1)
                for e in range(EA):
                    if e == 1:
                        pe.wait_ge(s["ffn_init"], b + 1)
                    output_layer(b, e)
                    if e + 2 < EA:
                        hidden_layer(e + 2)

        @block.scalar
        def _(act):
            a = nc.scalar.activation

            def move_x(n):
                act.wait_ge(s["xt_made"], n)
                a(xn_t[:, :], b_q[:, :], ACT.Copy).then_inc(s["xt_moved"], 1)
                a(xn_hi[:, :], b_q[:, :], ACT.Copy).then_inc(s["xhi_made"], 1)

            def move_values(k, made):
                act.wait_ge(s["val_made"], made)
                t = (k % 8) // 2
                a((vu, vp)[k // 8][:, t, 0:512], b_u[:, :], ACT.Copy).then_inc(s["val_moved_a"], 1)

            def move_projections(g1):
                act.wait_ge(s["u_made"], g1)
                a(qu_t[:, :], b_u[:, :], ACT.Copy).then_inc(s["u_moved"], 1)
                act.wait_ge(s["q_made"], g1)
                a(q_hi[:, :], b_q[:, :], ACT.Copy).then_inc(s["qhi_made"], 1)

            def tanh_logits(g1):
                act.wait_ge(s["quku_made"], g1)
                a(b_la[:, :], b_la[:, :], ACT.Tanh, scale=0.5).then_inc(s["tanh_la"], 1)

            def tanh_sums(g1):
                act.wait_ge(s["su_made"], g1)
                a(tanh_su[:, :, :], b_la[:, :].rearrange("p (t q) -> p t q", t=NT), ACT.Tanh, scale=-1.0)\
                    .then_inc(s["tanh_made"], 1)

            for k in range(0, 10, 2):
                act.wait_ge(s["wt_made"], k + 1)
                a(w_t[:, k // 2, 0:512], bank[k % 4][:, :], ACT.Copy).then_inc(s["wt_moved_a"], 1)
            for k in range(6):
                act.wait_ge(s["prod_made"], k + 1)
                hi = prod_dst[products[k // 2][0]][0]
                a(hi[:, (k % 2) * 512:(k % 2) * 512 + 512], bank[k][:, :], ACT.Copy,
                  scale=1.0 if k >= 4 else SCALE).then_inc(s["prod_hi"], 1)
            act.wait_ge(s["w_loaded"], 16 * 7)
            a(wu_hi[:, :], w_raw[:, 2048:3072], ACT.Copy).then_inc(s["wu_hi_made"], 1)
            act.wait_ge(s["ffn_loaded"], 16 * 9)
            a(w1_hi[:, :, :], w1_raw, ACT.Copy).then_inc(s["w1_hi_made"], 1)
            act.wait_ge(s["b1_made"], 1)
            a(b1[:, :], bank[6][:, 0:EA], ACT.Copy).then_inc(s["b1_moved"], 1)
            move_x(1)
            act.wait_ge(s["splits_made"], 3)
            for k in range(0, 16, 2):
                move_values(k, k + 1)
            move_projections(1)
            tanh_logits(1)
            tanh_sums(1)

            with act.Fori(0, B) as b:
                for h in range(H):
                    g0 = H * b + h
                    for n, i in enumerate(ROWS):
                        act.wait_ge(s["row_maxed"], 4 * g0 + n + 1)
                        w = (i + 1) * P
                        a(probs[:, i, 0:w], probs[:, i, 0:w], ACT.Exp, bias=neg_max[:, i:i + 1], scale=-1.0,
                          accum_out=row_sum[:, i:i + 1]).then_inc(s["row_exped"], 1)
                    if h < H - 1:
                        move_projections(g0 + 2)
                        tanh_logits(g0 + 2)
                    for n, rows in enumerate(([3], [2, 0], [1])):
                        act.wait_ge(s["pt_made"], 3 * g0 + n + 1)
                        at = 0
                        for i in rows:
                            last = a(probs_t[h % 2][:, 0:i + 1, i * P:(i + 1) * P],
                                     b_pt[n % 2][:, at:at + (i + 1) * P].rearrange("p (j q) -> p j q", q=P), ACT.Copy)
                            at += (i + 1) * P
                        last.then_inc(s["pt_moved"], 1)
                    if h < H - 1:
                        tanh_sums(g0 + 2)
                move_x(b + 2)
                for k in range(0, 16, 2):
                    move_values(k, 16 * b + 17 + k)
                act.wait_ge(s["yt_made"], b + 1)
                a(y_t[:, :], b_pt[1][:, :], ACT.Copy).then_inc(s["yt_moved"], 1)
                a(y_hi[:, :], b_pt[1][:, :], ACT.Copy).then_inc(s["yhi_made"], 1)
                move_projections(H * b + H + 1)
                tanh_logits(H * b + H + 1)
                act.wait_ge(s["logits_shifted"], b + 1)
                a(gates[:, :, :], logits[:, :, :], ACT.Exp).then_inc(s["gates_exped"], 1)

                def relu(e):
                    act.wait_ge(s["hid_made"], EA * b + e + 1)
                    a(hidden[e % 2][:, :], b_rows[e % 2][:, :], ACT.Relu, bias=b1[:, e:e + 1]).then_inc(s["hid_ready"], 1)

                relu(0)
                relu(1)
                tanh_sums(H * b + H + 1)
                act.wait_ge(s["cwt_made"], b + 1)
                a(cw_t[:, :], b_pt[0][0:EA, :], ACT.Copy).then_inc(s["cwt_moved"], 1)
                for e in range(2, EA):
                    relu(e)

        @block.vector
        def _(dve):
            v = nc.vector
            norm_count, row_count = dve.alloc_register("norm_count"), dve.alloc_register("row_count")
            dve.reg_mov(norm_count, 0)
            dve.reg_mov(row_count, 0)

            def norm_stats(tiles):
                for t in range(NT):
                    last = v.bn_stats(stats[:, t, :], tiles[t])
                last.then_inc(s["stats_made"], 1)
                dve.reg_add(norm_count, norm_count, 1)
                dve.wait_ge(s["consts_made"], 9)
                dve.wait_ge(s["stats_made"], norm_count)
                for t in range(NT):
                    last = v.bn_aggr(mv[:, t, :], stats[:, t, :])
                last.then_inc(s["mv_made"], 1)
                dve.wait_ge(s["mv_made"], norm_count)
                v.tensor_scalar(var_eps[:, :], mv[:, :, 1], EPS, None, ALU.add).then_inc(s["var_ready"], 1)

            def normalise(n, dst, tiles):
                dve.wait_ge(s["rstd_ready"], n)
                for t in range(NT):
                    last = v.tensor_scalar(dst[:, t, :], tiles[t], mv[:, t, 0:1], rstd[:, t:t + 1],
                                           ALU.subtract, ALU.mult)
                return last

            def low_part(dst, src, hi):
                return v.tensor_tensor(dst, src, hi.bitcast(F32), ALU.subtract)

            def x_low(n):
                dve.wait_ge(s["xhi_made"], n)
                low_part(xn_lo[:, :], b_q[:, :], xn_hi[:, :]).then_inc(s["xlo_made"], 1)

            def move_values(k, made):
                dve.wait_ge(s["val_made"], made)
                t = (k % 8) // 2
                v.tensor_copy((vu, vp)[k // 8][:, t, 512:1024], b_la[:, :]).then_inc(s["val_moved_v"], 1)

            def q_low(g1):
                dve.wait_ge(s["qhi_made"], g1)
                low_part(q_lo[:, :], b_q[:, :], q_hi[:, :]).then_inc(s["qlo_made"], 1)

            def lookahead(g1):
                dve.wait_ge(s["tanh_la"], g1)
                v.scalar_tensor_tensor(la_t[:, :, :], b_la[:, :].rearrange("p (t q) -> p t q", t=NT), 1.0,
                                       quarter[:, :, :], ALU.add, ALU.mult).then_inc(s["la_made"], 1)

            def silu(g1):
                dve.wait_ge(s["tanh_made"], g1)
                v.scalar_tensor_tensor(diag, tanh_su[:, :, :], 1.0, b_la[:, :].rearrange("p (t q) -> p t q", t=NT),
                                       ALU.subtract, ALU.mult).then_inc(s["silu_made"], 1)

            dve.wait_ge(s["x_loaded"], 16)
            dve.wait_ge(s["consts_made"], 9)
            x_tiles = [x_in[:, t, :] for t in range(NT)]
            norm_stats(x_tiles)
            normalise(1, xn, x_tiles).then_inc(s["xn_ready"], 1)
            for k in range(1, 10, 2):
                dve.wait_ge(s["wt_made"], k + 1)
                v.tensor_copy(w_t[:, k // 2, 512:1024], bank[k % 4][:, :]).then_inc(s["wt_moved_v"], 1)
            for k in range(6):
                dve.wait_ge(s["prod_hi"], k + 1)
                hi, lo = prod_dst[products[k // 2][0]]
                c = slice((k % 2) * 512, (k % 2) * 512 + 512)
                v.scalar_tensor_tensor(lo[:, c], bank[k][:, :], 1.0 if k >= 4 else SCALE, hi[:, c].bitcast(F32),
                                       ALU.mult, ALU.subtract).then_inc(s["prod_lo"], 1)
            dve.wait_ge(s["wu_hi_made"], 1)
            low_part(wu_lo[:, :], w_raw[:, 2048:3072], wu_hi[:, :]).then_inc(s["splits_made"], 1)
            dve.wait_ge(s["w1_hi_made"], 1)
            low_part(w1_lo[:, :, :], w1_raw, w1_hi[:, :, :]).then_inc(s["splits_made"], 1)
            v.memset(neg_silu, 0.0).then_inc(s["splits_made"], 1)
            x_low(1)
            for k in range(1, 16, 2):
                move_values(k, k + 1)
            q_low(1)
            lookahead(1)
            silu(1)

            with dve.Fori(0, B) as b:
                def max_row(n, g0):
                    i = ROWS[n]
                    w = (i + 1) * P
                    dve.reg_add(row_count, row_count, 1)
                    dve.wait_ge(s["consts_made"], 9)
                    dve.wait_ge(s["row_made"], row_count)
                    v.tensor_tensor_reduce(out=probs[:, i, 0:w], in0=b_rows[n % 2][:, 0:w], in1=neg_silu[:, i, 0:w],
                                           scale=-1.0, scalar=BIG, op0=ALU.add, op1=ALU.min,
                                           accum_out=neg_max[:, i:i + 1]).then_inc(s["row_maxed"], 1)

                def invert_sum(n, g0):
                    i = ROWS[n]
                    dve.wait_ge(s["row_exped"], 4 * g0 + n + 1)
                    v.reciprocal(row_inv[:, i:i + 1], row_sum[:, i:i + 1]).then_inc(s["inv_made"], 1)

                for h in range(H):
                    g0 = H * b + h
                    dve.wait_ge(s["silu_masked"], g0 + 1)
                    max_row(0, g0)
                    max_row(1, g0)
                    invert_sum(0, g0)
                    max_row(2, g0)
                    invert_sum(1, g0)
                    max_row(3, g0)
                    invert_sum(2, g0)
                    invert_sum(3, g0)
                    if h == 2:
                        dve.wait_ge(s["x_loaded"], 16 * b + 32)
                        norm_stats(x_tiles)
                    if h == 3:
                        normalise(4 * b + 2, xn, x_tiles).then_inc(s["xn_ready"], 1)
                    if h < H - 1:
                        q_low(g0 + 2)
                        lookahead(g0 + 2)
                        silu(g0 + 2)

                x_low(b + 2)
                move_values(1, 16 * b + 18)
                dve.wait_ge(s["att_made"], b + 1)
                v.tensor_copy(att_t[:, :], b_att[:, :]).then_inc(s["att_moved"], 1)
                for k in (3, 5, 7):
                    move_values(k, 16 * b + 17 + k)
                dve.wait_ge(s["atok_made"], b + 1)
                att_tiles = [b_pt[0][:, t * P:(t + 1) * P] for t in range(NT)]
                norm_stats(att_tiles)
                move_values(9, 16 * b + 26)
                normalise(4 * b + 3, normed, att_tiles).then_inc(s["normed_made"], 1)
                dve.wait_ge(s["res_loaded"], 16 * b + 16)
                dve.wait_ge(s["normed_made"], 2 * b + 1)
                v.tensor_tensor(x1[:, :, :], normed[:, :, :], x_res[:, :, :], ALU.add).then_inc(s["x1_ready"], 1)
                move_values(11, 16 * b + 28)
                dve.wait_ge(s["x1_ready"], b + 1)
                x1_tiles = [x1[:, t, :] for t in range(NT)]
                norm_stats(x1_tiles)
                move_values(13, 16 * b + 30)
                normalise(4 * b + 4, x1n, x1_tiles).then_inc(s["x1n_ready"], 1)
                move_values(15, 16 * b + 32)
                dve.wait_ge(s["yhi_made"], b + 1)
                low_part(y_lo[:, :], b_pt[1][:, :], y_hi[:, :]).then_inc(s["ylo_made"], 1)
                q_low(H * b + H + 1)
                dve.wait_ge(s["logits_made"], b + 1)
                raw = b_pt[0][:, 0:NT * 16].rearrange("p (t e) -> p t e", t=NT)[:, :, 0:E]
                steps = [0]

                def step(ins):
                    ins.then_inc(s["route_step"], 1)
                    steps[0] += 1
                    dve.wait_ge(s["route_step"], ROUTE_STEPS * b + steps[0])

                wide = [P, NT, E]
                step(v.tensor_reduce(top[:, :], raw, AX.X, ALU.max))
                v.tensor_tensor(logits[:, :, :], raw, top[:, :].unsqueeze(2).to_broadcast(wide), ALU.subtract)\
                    .then_inc(s["logits_shifted"], 1)
                lookahead(H * b + H + 1)
                dve.wait_ge(s["gates_exped"], b + 1)
                step(v.tensor_reduce(route_sum[:, :], gates[:, :, :], AX.X, ALU.add))
                step(v.reciprocal(route_inv[:, :], route_sum[:, :]))
                step(v.tensor_tensor(gates[:, :, :], gates[:, :, :], route_inv[:, :].unsqueeze(2).to_broadcast(wide), ALU.mult))
                pairs = [P, NT, E, E]
                mine, other = gates[:, :, :].unsqueeze(3).to_broadcast(pairs), gates[:, :, :].unsqueeze(2).to_broadcast(pairs)
                v.tensor_tensor(above[:, :, :, :], other, mine, ALU.is_gt)
                step(v.tensor_tensor(tied[:, :, :, :], other, mine, ALU.is_equal))
                step(v.tensor_tensor(tied[:, :, :, :], tied[:, :, :, :], lower[:, :, :].unsqueeze(1).to_broadcast(pairs), ALU.mult))
                step(v.tensor_tensor(above[:, :, :, :], above[:, :, :, :], tied[:, :, :, :], ALU.add))
                step(v.tensor_reduce(rank[:, :, :], above[:, :, :, :], AX.X, ALU.add))
                v.scalar_tensor_tensor(cw[:, :, 0:E], rank[:, :, :], float(TOPK), gates[:, :, :], ALU.is_lt, ALU.mult)\
                    .then_inc(s["cw_ready"], 1)
                assert steps[0] == ROUTE_STEPS
                silu(H * b + H + 1)
                dve.wait_ge(s["bias_made"], b + 1)
                v.tensor_copy(ffn[:, :, :], b_pt[1][:, :].rearrange("p (t n) -> p t n", t=NT)).then_inc(s["ffn_init"], 1)
                dve.wait_ge(s["ffn_init"], b + 1)
                for e in range(EA):
                    dve.wait_ge(s["ye_made"], EA * b + e + 1)
                    if e:
                        dve.wait_ge(s["ye_added"], EA * b + e)
                    for t in range(NT):
                        last = v.scalar_tensor_tensor(ffn[:, t, :], b_pt[e % 2][:, t * P:(t + 1) * P], cw[:, t, e:e + 1],
                                                      ffn[:, t, :], ALU.mult, ALU.add)
                    last.then_inc(s["ye_added"], 1)
                dve.wait_ge(s["ye_added"], EA * b + EA)
                ffn_tiles = [ffn[:, t, :] for t in range(NT)]
                norm_stats(ffn_tiles)
                normalise(4 * b + 5, normed, ffn_tiles).then_inc(s["normed_made"], 1)
                dve.wait_ge(s["normed_made"], 2 * b + 2)
                dve.wait_ge(s["stored"], 16 * b + 16)
                v.tensor_tensor(result[:, :, :], normed[:, :, :], x1[:, :, :], ALU.add).then_inc(s["result_ready"], 1)


_INS = ["x", "w_qkv", "w_out", "router_W", "router_b", "sW1", "sb1", "sW2", "sb2", "eW1", "eb1", "eW2", "eb2"]


def kernel(**inputs):
    import numpy as np
    import concourse.bacc as bacc
    from concourse.bass_utils import run_bass_kernel_spmd

    nc = bacc.Bacc("TRN2", target_bir_lowering=False, num_devices=1)
    arrays, args = {}, []
    for n in _INS:
        a = np.ascontiguousarray(inputs[("L0_attn_" if n in _INS[:3] else "L0_ffn_") + n])
        arrays[f"in_{n}"] = a
        args.append(nc.dram_tensor(f"in_{n}", a.shape, F32, kind="ExternalInput").ap())
    args.append(nc.dram_tensor("out", (B, S, D), F32, kind="ExternalOutput").ap())
    castle_moe(nc, *args)
    return run_bass_kernel_spmd(nc, [arrays], core_ids=[0]).results[0]["out"]
```

```python
import concourse.bass as bass
from concourse import mybir
from contextlib import ExitStack

P = 128
B, S, D = 8, 512, 128
H = 8
NT = S // P
E = 15
EA = E + 1
TOPK = 3
SCALE = float(D) ** -0.5
EPS = 1e-5
MASKED = -1e30
BIG = 3e38
F32 = mybir.dt.float32
F32R = mybir.dt.float32r
NORM_HEAD = 5
FFN_HEAD = 4
ROWS = [3, 2, 1, 0]
QKVS = dict(qu=0, ku=1, vu=2, q=3, k=4, v=5)


def castle_moe(nc, x, w_qkv, w_out, router_w, router_b, s_w1, s_b1, s_w2, s_b2, e_w1, e_b1, e_w2, e_b2, out):
    ALU, ACT, AX = mybir.AluOpType, mybir.ActivationFunctionType, mybir.AxisListType
    ctx = ExitStack()
    with ctx:
        def sb(name, shape, dt=F32):
            return ctx.enter_context(nc.sbuf_tensor(name, shape, dt))

        def sem(name):
            return ctx.enter_context(nc.semaphore(name))

        values = sb("values", [P, 2, NT, H * D])
        vu, vp = values[:, 0], values[:, 1]
        w_raw = values[:, :, :, :].rearrange("p a t n -> p (a t n)")[:, 0:6 * H * D]
        work = sb("work", [P, 7168])
        w_t = work[:, 0:5 * 1024].rearrange("p (m n) -> p m n", m=5)
        w1_raw = work[:, 5 * 1024:7 * 1024].rearrange("p (e n) -> p e n", e=EA)
        probs = work[:, 0:2048].rearrange("p (i j) -> p i j", i=NT)
        neg_silu_all = sb("neg_silu", [P, 2 * NT * S + NT * P])
        neg_silu = [neg_silu_all[:, 2048 * n:2048 * n + 2048].rearrange("p (i j) -> p i j", i=NT) for n in range(2)]
        diag = [neg_silu_all[:, 2048 * n:2048 * n + NT * (S + P)].rearrange("p (i j) -> p i j", j=S + P)[:, :, 0:P]
                for n in range(2)]
        probs_t = [work[:, 2048 + 2048 * n:4096 + 2048 * n].rearrange("p (j i) -> p j i", j=NT) for n in range(2)]
        wo_raw = sb("wo_raw", [P, H, D])
        mq_hi, mq_lo = sb("mq_hi", [P, H * D], F32R), sb("mq_lo", [P, H * D], F32R)
        mu_hi, mu_lo = sb("mu_hi", [P, H * D], F32R), sb("mu_lo", [P, H * D], F32R)
        wv_hi, wv_lo = sb("wv_hi", [P, H * D], F32R), sb("wv_lo", [P, H * D], F32R)
        wu_hi, wu_lo = sb("wu_hi", [P, H * D], F32R), sb("wu_lo", [P, H * D], F32R)
        w1_hi, w1_lo = sb("w1_hi", [P, EA, D], F32R), sb("w1_lo", [P, EA, D], F32R)
        w2 = sb("w2", [P, EA, D])
        b1_raw, b1 = sb("b1_raw", [EA, D]), sb("b1", [P, EA])
        b2 = sb("b2", [EA, D])
        rw, rb = sb("rw", [P, E]), sb("rb", [P, E])
        ident, quarter = sb("ident", [P, P]), sb("quarter", [P, NT, P])
        lower = sb("lower", [P, E, E])
        half_power = sb("half_power", [P, NT])
        x_in, x_res = sb("x_in", [P, NT, D]), sb("x_res", [P, NT, D])
        xn = sb("xn", [P, NT, D])
        xn_t, xn_hi, xn_lo = sb("xn_t", [P, S]), sb("xn_hi", [P, S], F32R), sb("xn_lo", [P, S], F32R)
        q_hi, q_lo, qu_t = sb("q_hi", [P, S], F32R), sb("q_lo", [P, S], F32R), sb("qu_t", [P, S])
        la_t, tanh_su = sb("la_t", [P, NT, P]), sb("tanh_su", [P, NT, P])
        neg_max, row_sum, row_inv = sb("neg_max", [P, NT]), sb("row_sum", [P, NT]), sb("row_inv", [P, NT])
        att_t = sb("att_t", [P, S])
        stats, mv = sb("stats", [P, NT, 6]), sb("mv", [P, NT, 2])
        var_eps, rstd = sb("var_eps", [P, NT]), sb("rstd", [P, NT])
        normed, x1, x1n = sb("normed", [P, NT, D]), sb("x1", [P, NT, D]), sb("x1n", [P, NT, D])
        y_t, y_hi, y_lo = sb("y_t", [P, S]), sb("y_hi", [P, S], F32R), sb("y_lo", [P, S], F32R)
        top, route_sum, route_inv = sb("top", [P, NT]), sb("route_sum", [P, NT]), sb("route_inv", [P, NT])
        logits, gates = sb("logits", [P, NT, E]), sb("gates", [P, NT, E])
        above, ties, rank = sb("above", [P, NT, E]), sb("ties", [P, NT, E]), sb("rank", [P, NT, E])
        tied, top8, n_above = sb("tied", [P, NT, E, E]), sb("top8", [P, NT, 8]), sb("n_above", [P, NT])
        cw, cw_t = sb("cw", [P, NT, EA]), sb("cw_t", [EA, S])
        hidden = [sb(f"hidden{n}", [P, S]) for n in range(2)]
        ffn, result = sb("ffn", [P, NT, D]), sb("result", [P, NT, D])

        bank = [ctx.enter_context(nc.psum_tensor(f"bank{n}", [P, 512], F32)) for n in range(8)]
        b_att, b_q, b_u, b_la = bank[0], bank[1], bank[2], bank[3]
        b_rows, b_pt = bank[4:6], bank[6:8]

        names = """w_loaded x_loaded ffn_loaded res_loaded consts_made stored
            wt_made wt_moved_a wt_moved_v prod_made prod_hi prod_lo wu_hi_made w1_hi_made splits_made b1_made b1_moved
            xn_ready xt_made xt_moved xhi_made xlo_made x1_ready val_made val_moved_a val_moved_v
            q_made u_made qhi_made qlo_made u_moved quku_made tanh_la la_made su_made tanh_made silu_made silu_masked
            row_made row_maxed row_exped inv_made row_normed pt_made pt_moved att_made att_moved atok_made
            stats_made mv_made var_ready rstd_ready x1n_ready normed_made yt_made yt_moved yhi_made ylo_made
            logits_made logits_shifted gates_exped route_step ties_ready ties_masked cw_ready cwt_made cwt_moved bias_made ffn_init
            hid_made hid_ready ye_made ye_added result_ready""".split()
        s = {n: sem(n) for n in names}

        block = ctx.enter_context(nc.Block())
        xv = x.rearrange("b (t p) d -> b p t d", p=P)
        ov = out.rearrange("b (t p) d -> b p t d", p=P)
        order = ["qu", "ku", "q", "k", "v"]
        products = [("mu", 0, 1), ("mq", 2, 3), ("wv", 4, None)]
        prod_dst = dict(mu=(mu_hi, mu_lo), mq=(mq_hi, mq_lo), wv=(wv_hi, wv_lo))

        @block.sync
        def _(sp):
            sp.dma_start(x_in[:, :, :], xv[0]).then_inc(s["x_loaded"], 16)
            for n in range(6):
                sp.dma_start(w_raw[:, n * 1024:(n + 1) * 1024], w_qkv[:, n * 1024:(n + 1) * 1024]).then_inc(s["w_loaded"], 16)
            sp.dma_start(wo_raw[:, :, :], w_out.rearrange("(h p) n -> p h n", p=P)).then_inc(s["w_loaded"], 16)
            sp.dma_start(w1_raw[:, 0:E, :], e_w1.rearrange("e d n -> d e n")).then_inc(s["ffn_loaded"], 16)
            sp.dma_start(w1_raw[:, E, :], s_w1).then_inc(s["ffn_loaded"], 16)
            sp.dma_start(w2[:, 0:E, :], e_w2.rearrange("e d n -> d e n")).then_inc(s["ffn_loaded"], 16)
            sp.dma_start(w2[:, E, :], s_w2).then_inc(s["ffn_loaded"], 16)
            sp.dma_start(b1_raw[0:E, :], e_b1).then_inc(s["ffn_loaded"], 16)
            sp.dma_start(b1_raw[E:EA, :], s_b1.rearrange("(a n) -> a n", a=1)).then_inc(s["ffn_loaded"], 16)
            sp.dma_start(b2[0:E, :], e_b2).then_inc(s["ffn_loaded"], 16)
            sp.dma_start(b2[E:EA, :], s_b2.rearrange("(a n) -> a n", a=1)).then_inc(s["ffn_loaded"], 16)
            sp.dma_start(rw[:, :], router_w).then_inc(s["ffn_loaded"], 16)
            sp.dma_start(rb[:, :], router_b.partition_broadcast(P)).then_inc(s["stored"], 16)

            def batch(b, after, b_res):
                if after is not None:
                    sp.wait_ge(s["xn_ready"], b + 1)
                    sp.dma_start(x_in[:, :, :], xv[after]).then_inc(s["x_loaded"], 16)
                if b_res is not None:
                    sp.wait_ge(s["x1_ready"], b_res)
                sp.dma_start(x_res[:, :, :], xv[b]).then_inc(s["res_loaded"], 16)
                sp.wait_ge(s["result_ready"], b + 1)
                sp.dma_start(ov[b], result[:, :, :]).then_inc(s["stored"], 16)

            batch(0, 1, None)
            with sp.Fori(1, B - 1) as b:
                batch(b, b + 1, b)
            batch(B - 1, None, B - 1)
            sp.wait_ge(s["stored"], 16 * (B + 1))

        @block.gpsimd
        def _(pool):
            g = nc.gpsimd
            silu_count, row_count = pool.alloc_register("silu_count"), pool.alloc_register("row_count")
            pool.reg_mov(silu_count, 0)
            pool.reg_mov(row_count, 0)
            g.memset(ident[:, :], 0.0).then_inc(s["consts_made"], 1)
            g.memset(quarter[:, :, :], 0.25).then_inc(s["consts_made"], 1)
            g.memset(lower[:, :, :], 1.0).then_inc(s["consts_made"], 1)
            g.memset(half_power[:, :], -0.5).then_inc(s["consts_made"], 1)
            g.memset(cw[:, :, E:EA], 1.0).then_inc(s["consts_made"], 1)
            pool.wait_ge(s["consts_made"], 5)
            g.affine_select(out=ident[:, :], in_=ident[:, :], compare_op=ALU.not_equal, fill=1.0, base=0,
                            pattern=[[-1, P]], channel_multiplier=1).then_inc(s["consts_made"], 1)
            g.affine_select(out=quarter[:, :, :], in_=quarter[:, :, :], compare_op=ALU.is_gt, fill=0.0, base=0,
                            pattern=[[0, NT], [-1, P]], channel_multiplier=1).then_inc(s["consts_made"], 1)
            g.affine_select(out=lower[:, :, :], in_=lower[:, :, :], compare_op=ALU.is_gt, fill=0.0, base=0,
                            pattern=[[1, E], [-1, E]], channel_multiplier=0).then_inc(s["consts_made"], 1)

            def inv_sqrt(n):
                pool.wait_ge(s["var_ready"], n)
                g.tensor_tensor(rstd[:, :], var_eps[:, :], half_power[:, :], ALU.pow).then_inc(s["rstd_ready"], 1)

            def mask_silu(h):
                pool.reg_add(silu_count, silu_count, 1)
                pool.wait_ge(s["consts_made"], 8)
                pool.wait_ge(s["silu_made"], silu_count)
                g.affine_select(out=diag[h % 2], in_=diag[h % 2], compare_op=ALU.is_ge, fill=MASKED, base=0,
                                pattern=[[0, NT], [-1, P]], channel_multiplier=1).then_inc(s["silu_masked"], 1)

            def head(b, h, masks=True):
                for n, i in enumerate(ROWS):
                    pool.reg_add(row_count, row_count, 1)
                    pool.wait_ge(s["consts_made"], 8)
                    pool.wait_ge(s["inv_made"], row_count)
                    w = (i + 1) * P
                    g.tensor_scalar(probs[:, i, 0:w], probs[:, i, 0:w], row_inv[:, i:i + 1], 1.0,
                                    ALU.mult, ALU.mult).then_inc(s["row_normed"], 1)
                if masks:
                    mask_silu(h + 1)

            def mask_ties(b):
                pool.wait_ge(s["ties_ready"], b + 1)
                pairs = [P, NT, E, E]
                g.tensor_tensor(tied[:, :, :, :], ties[:, :, :].unsqueeze(2).to_broadcast(pairs),
                                lower[:, :, :].unsqueeze(1).to_broadcast(pairs), ALU.mult).then_inc(s["ties_masked"], 1)

            inv_sqrt(1)
            mask_silu(0)
            for h in range(FFN_HEAD + 1):
                head(0, h)
            with pool.Fori(0, B - 1) as b:
                for h in range(FFN_HEAD + 1, H):
                    head(b, h, masks=h < H - 1)
                    if h == NORM_HEAD:
                        inv_sqrt(4 * b + 2)
                mask_silu(0)
                inv_sqrt(4 * b + 3)
                for h in range(FFN_HEAD + 1):
                    head(b + 1, h)
                    if h == 0:
                        inv_sqrt(4 * b + 4)
                    if h == 2:
                        mask_ties(b)
                inv_sqrt(4 * b + 5)
            for h in range(FFN_HEAD + 1, H):
                head(B - 1, h, masks=h < H - 1)
            inv_sqrt(4 * B - 2)
            inv_sqrt(4 * B - 1)
            mask_ties(B - 1)
            inv_sqrt(4 * B)

        @block.tensor
        def _(pe):
            mm = nc.tensor.matmul

            def mm3(dst, a_hi, a_lo, c_hi, c_lo, start=True, stop=True):
                mm(dst, a_lo, c_hi, start=start, stop=False)
                mm(dst, a_hi, c_lo, start=False, stop=False)
                return mm(dst, a_hi, c_hi, start=False, stop=stop)

            def tile(t):
                return slice(t * P, (t + 1) * P)

            def transpose_x():
                for t in range(NT):
                    last = nc.tensor.transpose(b_q[:, tile(t)], xn[:, t, :], ident[:, :])
                last.then_inc(s["xt_made"], 1)

            def value_group(k, b):
                if k >= 2:
                    if k >= 10:
                        pe.wait_ge(s["val_moved_a"], 12 * b + k - 5)
                    elif k % 2 == 0:
                        pe.wait_ge(s["val_moved_a"], 12 * b + k // 2)
                    else:
                        pe.wait_ge(s["val_moved_v"], 4 * b + k // 2)
                hi, lo = ((wu_hi, wu_lo), (wv_hi, wv_lo))[k // 8]
                t, half = (k % 8) // 2, k % 2
                c = slice(half * 512, half * 512 + 512)
                mm3(b_rows[k % 2][:, :], xn_hi[:, tile(t)], xn_lo[:, tile(t)], hi[:, c], lo[:, c]).then_inc(s["val_made"], 1)

            def project_u(h):
                c = slice(h * D, (h + 1) * D)
                mm3(b_u[:, :], mu_hi[:, c], mu_lo[:, c], xn_hi[:, :], xn_lo[:, :]).then_inc(s["u_made"], 1)

            def project_q(h):
                c = slice(h * D, (h + 1) * D)
                mm3(b_q[:, :], mq_hi[:, c], mq_lo[:, c], xn_hi[:, :], xn_lo[:, :]).then_inc(s["q_made"], 1)

            def lookahead_logits(g1):
                pe.wait_ge(s["u_moved"], g1)
                if not isinstance(g1, int) or g1 > 1:
                    pe.wait_ge(s["silu_made"], g1 - 1)
                for t in range(NT):
                    last = mm(b_la[:, tile(t)], xn_t[:, tile(t)], qu_t[:, tile(t)], start=True, stop=True)
                last.then_inc(s["quku_made"], 1)

            def lookahead_sum(h, g1):
                pe.wait_ge(s["la_made"], g1)
                for t in range(NT):
                    last = mm(b_la[:, tile(t)], la_t[:, t, :], vu[:, t, h * D:(h + 1) * D], start=True, stop=True)
                last.then_inc(s["su_made"], 1)

            def score_row(n):
                i = ROWS[n]
                w = (i + 1) * P
                mm3(b_rows[n % 2][:, 0:w], q_hi[:, tile(i)], q_lo[:, tile(i)], xn_hi[:, 0:w], xn_lo[:, 0:w])\
                    .then_inc(s["row_made"], 1)

            def transpose_rows(rows, dst, signal=True):
                at = 0
                for i in rows:
                    for j in range(i + 1):
                        last = nc.tensor.transpose(dst[:, at:at + P], probs[:, i, tile(j)], ident[:, :])
                        at += P
                last.then_inc(s["pt_made"], 1)

            def attend(h, j):
                return mm(b_att[:, j * P:S], vp[:, j, h * D:(h + 1) * D], probs_t[h % 2][:, j, j * P:S],
                          start=(h == 0 and j == 0), stop=(h == H - 1 and j == NT - 1), skip_group_check=True)

            def hidden_layer(e):
                mm3(b_rows[e % 2][:, :], w1_hi[:, e, :], w1_lo[:, e, :], y_hi[:, :], y_lo[:, :]).then_inc(s["hid_made"], 1)

            def output_layer(b, e):
                pe.wait_ge(s["hid_ready"], EA * b + e + 1)
                if e == 1:
                    pe.wait_ge(s["ffn_init"], b + 1)
                if e >= 2:
                    pe.wait_ge(s["ye_added"], EA * b + e - 1)
                for t in range(NT):
                    last = mm(b_pt[e % 2][:, tile(t)], hidden[e % 2][:, tile(t)], w2[:, e, :], start=True, stop=True)
                last.then_inc(s["ye_made"], 1)

            pe.wait_ge(s["consts_made"], 8)
            for k in range(10):
                m, half = k // 2, k % 2
                if k == 0:
                    pe.wait_ge(s["w_loaded"], 16 * 7)
                if k >= 4:
                    pe.wait_ge(s["wt_moved_a" if k % 2 == 0 else "wt_moved_v"], (k - 4) // 2 + 1)
                for n in range(4):
                    h = half * 4 + n
                    c = QKVS[order[m]] * 1024 + h * D
                    last = nc.tensor.transpose(bank[k % 4][:, tile(n)], w_raw[:, c:c + D], ident[:, :])
                last.then_inc(s["wt_made"], 1)
            pe.wait_ge(s["wt_moved_a"], 5)
            pe.wait_ge(s["wt_moved_v"], 5)
            k = 0
            for name, left, right in products:
                for half in range(2):
                    for n in range(4):
                        h = half * 4 + n
                        rhs = wo_raw[:, h, :] if right is None else w_t[:, right, h * D:(h + 1) * D]
                        last = mm(bank[k][:, tile(n)], w_t[:, left, h * D:(h + 1) * D], rhs, start=True, stop=True)
                    last.then_inc(s["prod_made"], 1)
                    k += 1
            pe.wait_ge(s["ffn_loaded"], 16 * 9)
            nc.tensor.transpose(bank[6][:, 0:EA], b1_raw[:, :], ident[0:EA, 0:EA]).then_inc(s["b1_made"], 1)

            def head(b, h, finishing=None):
                g0 = H * b + h
                pe.wait_ge(s["qlo_made"], g0 + 1)
                score_row(0)
                score_row(1)
                if h < H - 1:
                    lookahead_logits(g0 + 2)
                if h:
                    pe.wait_ge(s["pt_moved"], 3 * g0)
                    attend(h - 1, 0)
                if finishing is not None and h == 2:
                    router_logits(finishing)
                pe.wait_ge(s["row_maxed"], 4 * g0 + 1)
                score_row(2)
                pe.wait_ge(s["row_maxed"], 4 * g0 + 2)
                score_row(3)
                if h == H - 1 and not isinstance(b, int):
                    pe.wait_ge(s["xn_ready"], b + 2)
                    transpose_x()
                if h:
                    attend(h - 1, 1)
                if h < H - 1:
                    lookahead_sum(h + 1, g0 + 2)
                    project_q(h + 1)
                if finishing is not None and h == 2:
                    pe.wait_ge(s["logits_shifted"], finishing + 1)
                pe.wait_ge(s["row_normed"], 4 * g0 + 1)
                transpose_rows([3], b_pt[0])
                pe.wait_ge(s["row_normed"], 4 * g0 + 4)
                transpose_rows([2, 0], b_pt[1])
                if finishing is not None and h == 1:
                    transpose_x1n(finishing, b_u)
                late_u = finishing is not None and h == 1
                if h < H - 2 and not late_u:
                    project_u(h + 2)
                if h:
                    attend(h - 1, 2)
                    attend(h - 1, 3)
                pe.wait_ge(s["pt_moved"], 3 * g0 + 1)
                transpose_rows([1], b_pt[0])
                if late_u:
                    pe.wait_ge(s["ylo_made"], finishing + 1)
                    project_u(h + 2)

            def transpose_x1n(b, dst):
                pe.wait_ge(s["x1n_ready"], b + 1)
                for t in range(NT):
                    last = nc.tensor.transpose(dst[:, tile(t)], x1n[:, t, :], ident[:, :])
                last.then_inc(s["yt_made"], 1)

            def router_logits(b):
                pe.wait_ge(s["ylo_made"], b + 1)
                for t in range(NT):
                    c = slice(t * 16, t * 16 + E)
                    last = mm(b_u[:, c], y_t[:, tile(t)], rw[:, :], start=True, stop=True)
                last.then_inc(s["logits_made"], 1)

            def experts(b, projected=None):
                hidden_layer(0)
                hidden_layer(1)
                pe.wait_ge(s["cw_ready"], b + 1)
                if projected is not None:
                    pe.wait_ge(s["u_moved"], projected)
                for t in range(NT):
                    last = nc.tensor.transpose(b_u[0:EA, tile(t)], cw[:, t, :], ident[:, :])
                last.then_inc(s["cwt_made"], 1)
                pe.wait_ge(s["cwt_moved"], b + 1)
                for t in range(NT):
                    last = mm(b_pt[1][:, tile(t)], cw_t[:, tile(t)], b2[:, :], start=True, stop=True)
                last.then_inc(s["bias_made"], 1)
                for e in range(EA):
                    output_layer(b, e)
                    if e + 2 < EA:
                        hidden_layer(e + 2)

            def attend_last(b):
                pe.wait_ge(s["pt_moved"], 3 * (H * b + H))
                for j in range(NT):
                    last = attend(H - 1, j)
                last.then_inc(s["att_made"], 1)

            def attention_tokens(b):
                pe.wait_ge(s["att_moved"], b + 1)
                for t in range(NT):
                    last = nc.tensor.transpose(b_pt[0][:, tile(t)], att_t[:, tile(t)], ident[:, :])
                last.then_inc(s["atok_made"], 1)

            pe.wait_ge(s["xn_ready"], 1)
            pe.wait_ge(s["prod_lo"], 6)
            transpose_x()
            pe.wait_ge(s["xlo_made"], 1)
            pe.wait_ge(s["splits_made"], 1)
            for k in range(8):
                value_group(k, 0)
            project_u(0)
            project_q(0)
            lookahead_logits(1)
            for k in range(8, 12):
                value_group(k, 0)
            lookahead_sum(0, 1)
            project_u(1)
            for k in range(12, 16):
                value_group(k, 0)
            pe.wait_ge(s["val_moved_a"], 12)
            for h in range(FFN_HEAD + 1):
                head(0, h)

            with pe.Fori(0, B - 1) as b:
                for h in range(FFN_HEAD + 1, H):
                    head(b, h)
                pe.wait_ge(s["xlo_made"], b + 2)
                for k in range(4):
                    value_group(k, b + 1)
                attend_last(b)
                project_u(0)
                value_group(4, b + 1)
                project_q(0)
                value_group(5, b + 1)
                lookahead_logits(H * b + H + 1)
                value_group(6, b + 1)
                value_group(7, b + 1)
                attention_tokens(b)
                value_group(8, b + 1)
                lookahead_sum(0, H * b + H + 1)
                project_u(1)
                for k in range(9, 16):
                    value_group(k, b + 1)
                pe.wait_ge(s["val_moved_a"], 12 * b + 24)
                for h in range(FFN_HEAD):
                    head(b + 1, h, finishing=b)
                experts(b, H * (b + 1) + FFN_HEAD + 2)
                head(b + 1, FFN_HEAD)
            for h in range(FFN_HEAD + 1, H):
                head(B - 1, h)
            attend_last(B - 1)
            attention_tokens(B - 1)
            transpose_x1n(B - 1, b_u)
            router_logits(B - 1)
            experts(B - 1)

        @block.scalar
        def _(act):
            a = nc.scalar.activation

            def move_x(n):
                act.wait_ge(s["xt_made"], n)
                a(xn_t[:, :], b_q[:, :], ACT.Copy).then_inc(s["xt_moved"], 1)
                a(xn_hi[:, :], b_q[:, :], ACT.Copy).then_inc(s["xhi_made"], 1)

            def move_values(k, made):
                act.wait_ge(s["val_made"], made)
                t, half = (k % 8) // 2, k % 2
                a((vu, vp)[k // 8][:, t, half * 512:half * 512 + 512], b_rows[half][:, :], ACT.Copy).then_inc(s["val_moved_a"], 1)

            def move_u(g1):
                act.wait_ge(s["u_made"], g1)
                a(qu_t[:, :], b_u[:, :], ACT.Copy).then_inc(s["u_moved"], 1)

            def q_high(g1):
                act.wait_ge(s["q_made"], g1)
                a(q_hi[:, :], b_q[:, :], ACT.Copy).then_inc(s["qhi_made"], 1)

            def tanh_logits(g1):
                act.wait_ge(s["quku_made"], g1)
                a(b_la[:, :], b_la[:, :], ACT.Tanh, scale=0.5).then_inc(s["tanh_la"], 1)

            def tanh_sums(g1):
                act.wait_ge(s["su_made"], g1)
                a(tanh_su[:, :, :], b_la[:, :].rearrange("p (t q) -> p t q", t=NT), ACT.Tanh, scale=-1.0)\
                    .then_inc(s["tanh_made"], 1)

            for k in range(0, 10, 2):
                act.wait_ge(s["wt_made"], k + 1)
                a(w_t[:, k // 2, 0:512], bank[k % 4][:, :], ACT.Copy).then_inc(s["wt_moved_a"], 1)
            for k in range(6):
                act.wait_ge(s["prod_made"], k + 1)
                hi = prod_dst[products[k // 2][0]][0]
                a(hi[:, (k % 2) * 512:(k % 2) * 512 + 512], bank[k][:, :], ACT.Copy,
                  scale=1.0 if k >= 4 else SCALE).then_inc(s["prod_hi"], 1)
            act.wait_ge(s["w_loaded"], 16 * 7)
            a(wu_hi[:, :], w_raw[:, 2048:3072], ACT.Copy).then_inc(s["wu_hi_made"], 1)
            act.wait_ge(s["ffn_loaded"], 16 * 9)
            a(w1_hi[:, :, :], w1_raw, ACT.Copy).then_inc(s["w1_hi_made"], 1)
            act.wait_ge(s["b1_made"], 1)
            a(b1[:, :], bank[6][:, 0:EA], ACT.Copy).then_inc(s["b1_moved"], 1)
            move_x(1)
            act.wait_ge(s["splits_made"], 3)
            def head(b, h, finishing=None):
                g0 = H * b + h
                for n, i in enumerate(ROWS):
                    act.wait_ge(s["row_maxed"], 4 * g0 + n + 1)
                    w = (i + 1) * P
                    a(probs[:, i, 0:w], probs[:, i, 0:w], ACT.Exp, bias=neg_max[:, i:i + 1], scale=-1.0,
                      accum_out=row_sum[:, i:i + 1]).then_inc(s["row_exped"], 1)
                    if n == 0 and h < H - 1:
                        tanh_logits(g0 + 2)
                if h < H - 1:
                    tanh_sums(g0 + 2)
                    q_high(g0 + 2)
                elif not isinstance(b, int):
                    move_x(b + 2)
                if finishing is not None and h == 2:
                    exp_gates(finishing)
                late_u = finishing is not None and h == 1
                for n, rows in enumerate(([3], [2, 0], [1])):
                    if n == 2 and late_u:
                        move_x1n(finishing, b_u)
                    elif n == 2 and h < H - 2:
                        move_u(g0 + 3)
                    act.wait_ge(s["pt_made"], 3 * g0 + n + 1)
                    at = 0
                    for i in rows:
                        last = a(probs_t[h % 2][:, 0:i + 1, i * P:(i + 1) * P],
                                 b_pt[n % 2][:, at:at + (i + 1) * P].rearrange("p (j q) -> p j q", q=P), ACT.Copy)
                        at += (i + 1) * P
                    last.then_inc(s["pt_moved"], 1)
                if late_u:
                    move_u(g0 + 3)

            def move_x1n(b, src):
                act.wait_ge(s["yt_made"], b + 1)
                a(y_t[:, :], src[:, :], ACT.Copy).then_inc(s["yt_moved"], 1)
                a(y_hi[:, :], src[:, :], ACT.Copy).then_inc(s["yhi_made"], 1)

            def exp_gates(b):
                act.wait_ge(s["logits_shifted"], b + 1)
                a(gates[:, :, :], logits[:, :, :], ACT.Exp).then_inc(s["gates_exped"], 1)

            def relu(b, e):
                act.wait_ge(s["hid_made"], EA * b + e + 1)
                a(hidden[e % 2][:, :], b_rows[e % 2][:, :], ACT.Relu, bias=b1[:, e:e + 1]).then_inc(s["hid_ready"], 1)

            def experts(b):
                relu(b, 0)
                relu(b, 1)
                act.wait_ge(s["cwt_made"], b + 1)
                a(cw_t[:, :], b_u[0:EA, :], ACT.Copy).then_inc(s["cwt_moved"], 1)
                for e in range(2, EA):
                    relu(b, e)

            for k in range(0, 8, 2):
                move_values(k, k + 1)
            move_u(1)
            q_high(1)
            tanh_logits(1)
            for k in range(8, 12):
                move_values(k, k + 1)
            tanh_sums(1)
            move_u(2)
            for k in range(12, 16):
                move_values(k, k + 1)
            for h in range(FFN_HEAD + 1):
                head(0, h)

            with act.Fori(0, B - 1) as b:
                for h in range(FFN_HEAD + 1, H):
                    head(b, h)
                v0 = 16 * b + 17
                move_values(0, v0)
                move_values(2, v0 + 2)
                move_u(H * b + H + 1)
                move_values(4, v0 + 4)
                q_high(H * b + H + 1)
                tanh_logits(H * b + H + 1)
                move_values(6, v0 + 6)
                move_values(8, v0 + 8)
                tanh_sums(H * b + H + 1)
                move_u(H * b + H + 2)
                for k in range(9, 16):
                    move_values(k, v0 + k)
                for h in range(FFN_HEAD):
                    head(b + 1, h, finishing=b)
                experts(b)
                head(b + 1, FFN_HEAD)
            for h in range(FFN_HEAD + 1, H):
                head(B - 1, h)
            move_x1n(B - 1, b_u)
            exp_gates(B - 1)
            experts(B - 1)

        @block.vector
        def _(dve):
            v = nc.vector
            norm_count, row_count = dve.alloc_register("norm_count"), dve.alloc_register("row_count")
            step_count = dve.alloc_register("step_count")
            dve.reg_mov(norm_count, 0)
            dve.reg_mov(row_count, 0)

            def norm_stats(tiles):
                for t in range(NT):
                    last = v.bn_stats(stats[:, t, :], tiles[t])
                last.then_inc(s["stats_made"], 1)
                dve.reg_add(norm_count, norm_count, 1)
                dve.wait_ge(s["consts_made"], 8)
                dve.wait_ge(s["stats_made"], norm_count)
                for t in range(NT):
                    last = v.bn_aggr(mv[:, t, :], stats[:, t, :])
                last.then_inc(s["mv_made"], 1)
                dve.wait_ge(s["mv_made"], norm_count)
                v.tensor_scalar(var_eps[:, :], mv[:, :, 1], EPS, None, ALU.add).then_inc(s["var_ready"], 1)

            def normalise(n, dst, tiles):
                dve.wait_ge(s["rstd_ready"], n)
                for t in range(NT):
                    last = v.tensor_scalar(dst[:, t, :], tiles[t], mv[:, t, 0:1], rstd[:, t:t + 1],
                                           ALU.subtract, ALU.mult)
                return last

            def low_part(dst, src, hi):
                return v.tensor_tensor(dst, src, hi.bitcast(F32), ALU.subtract)

            def x_low(n):
                dve.wait_ge(s["xhi_made"], n)
                low_part(xn_lo[:, :], b_q[:, :], xn_hi[:, :]).then_inc(s["xlo_made"], 1)

            def move_values(k, made):
                dve.wait_ge(s["val_made"], made)
                t = (k % 8) // 2
                v.tensor_copy((vu, vp)[k // 8][:, t, 512:1024], b_rows[1][:, :]).then_inc(s["val_moved_v"], 1)

            def q_low(g1):
                dve.wait_ge(s["qhi_made"], g1)
                low_part(q_lo[:, :], b_q[:, :], q_hi[:, :]).then_inc(s["qlo_made"], 1)

            def lookahead(g1):
                dve.wait_ge(s["tanh_la"], g1)
                v.scalar_tensor_tensor(la_t[:, :, :], b_la[:, :].rearrange("p (t q) -> p t q", t=NT), 1.0,
                                       quarter[:, :, :], ALU.add, ALU.mult).then_inc(s["la_made"], 1)

            def silu(g1, h):
                dve.wait_ge(s["tanh_made"], g1)
                v.scalar_tensor_tensor(diag[h % 2], tanh_su[:, :, :], 1.0, b_la[:, :].rearrange("p (t q) -> p t q", t=NT),
                                       ALU.subtract, ALU.mult).then_inc(s["silu_made"], 1)

            dve.wait_ge(s["x_loaded"], 16)
            dve.wait_ge(s["consts_made"], 8)
            x_tiles = [x_in[:, t, :] for t in range(NT)]
            norm_stats(x_tiles)
            normalise(1, xn, x_tiles).then_inc(s["xn_ready"], 1)
            for k in range(1, 10, 2):
                dve.wait_ge(s["wt_made"], k + 1)
                v.tensor_copy(w_t[:, k // 2, 512:1024], bank[k % 4][:, :]).then_inc(s["wt_moved_v"], 1)
            for k in range(6):
                dve.wait_ge(s["prod_hi"], k + 1)
                hi, lo = prod_dst[products[k // 2][0]]
                c = slice((k % 2) * 512, (k % 2) * 512 + 512)
                v.scalar_tensor_tensor(lo[:, c], bank[k][:, :], 1.0 if k >= 4 else SCALE, hi[:, c].bitcast(F32),
                                       ALU.mult, ALU.subtract).then_inc(s["prod_lo"], 1)
            dve.wait_ge(s["wu_hi_made"], 1)
            low_part(wu_lo[:, :], w_raw[:, 2048:3072], wu_hi[:, :]).then_inc(s["splits_made"], 1)
            dve.wait_ge(s["w1_hi_made"], 1)
            low_part(w1_lo[:, :, :], w1_raw, w1_hi[:, :, :]).then_inc(s["splits_made"], 1)
            v.memset(neg_silu_all[:, :], 0.0).then_inc(s["splits_made"], 1)
            x_low(1)
            def max_row(n, h):
                i = ROWS[n]
                w = (i + 1) * P
                dve.reg_add(row_count, row_count, 1)
                dve.wait_ge(s["consts_made"], 8)
                dve.wait_ge(s["row_made"], row_count)
                v.tensor_tensor_reduce(out=probs[:, i, 0:w], in0=b_rows[n % 2][:, 0:w], in1=neg_silu[h % 2][:, i, 0:w],
                                       scale=-1.0, scalar=BIG, op0=ALU.add, op1=ALU.min,
                                       accum_out=neg_max[:, i:i + 1]).then_inc(s["row_maxed"], 1)

            def invert_sum(n, g0):
                i = ROWS[n]
                dve.wait_ge(s["row_exped"], 4 * g0 + n + 1)
                v.reciprocal(row_inv[:, i:i + 1], row_sum[:, i:i + 1]).then_inc(s["inv_made"], 1)

            def head(b, h, finishing=None, finished=None):
                g0 = H * b + h
                dve.wait_ge(s["silu_masked"], g0 + 1)
                max_row(0, h)
                max_row(1, h)
                invert_sum(0, g0)
                if h < H - 1:
                    lookahead(g0 + 2)
                invert_sum(1, g0)
                max_row(2, h)
                max_row(3, h)
                invert_sum(2, g0)
                invert_sum(3, g0)
                if h == NORM_HEAD and not isinstance(b, int):
                    dve.wait_ge(s["x_loaded"], 16 * b + 32)
                    norm_stats(x_tiles)
                if h == NORM_HEAD + 1 and not isinstance(b, int):
                    normalise(4 * b + 2, xn, x_tiles).then_inc(s["xn_ready"], 1)
                if finishing is not None and h == 0:
                    dve.wait_ge(s["x1_ready"], finishing + 1)
                    norm_stats(x1_tiles)
                if finishing is not None and h == 1:
                    normalise(4 * finishing + 4, x1n, x1_tiles).then_inc(s["x1n_ready"], 1)
                if finishing is not None and h == 2:
                    shift_logits(finishing)
                if finished is not None:
                    norm_stats(ffn_tiles)
                if h < H - 1:
                    silu(g0 + 2, h + 1)
                    q_low(g0 + 2)
                    if finishing is not None and h == 1:
                        x1n_low(finishing, b_u)
                elif not isinstance(b, int):
                    x_low(b + 2)
                if finishing is not None and h == 2:
                    route_softmax(finishing)
                    compare_gates()
                if finishing is not None and h == 3:
                    choose_experts(finishing)
                if finished is not None:
                    finish(finished, 4 * finished + 5)

            def x1n_low(b, src):
                dve.wait_ge(s["yhi_made"], b + 1)
                low_part(y_lo[:, :], src[:, :], y_hi[:, :]).then_inc(s["ylo_made"], 1)

            wide, pairs = [P, NT, E], [P, NT, E, E]

            dve.reg_mov(step_count, 0)

            def step(ins):
                ins.then_inc(s["route_step"], 1)
                dve.reg_add(step_count, step_count, 1)
                dve.wait_ge(s["consts_made"], 8)
                dve.wait_ge(s["route_step"], step_count)

            def shift_logits(b):
                dve.wait_ge(s["stored"], 16)
                dve.wait_ge(s["logits_made"], b + 1)
                raw = b_u[:, 0:NT * 16].rearrange("p (t e) -> p t e", t=NT)[:, :, 0:E]
                step(v.tensor_tensor(logits[:, :, :], raw, rb[:, :].unsqueeze(1).to_broadcast(wide), ALU.add))
                step(v.tensor_reduce(top[:, :], logits[:, :, :], AX.X, ALU.max))
                v.tensor_tensor(logits[:, :, :], logits[:, :, :], top[:, :].unsqueeze(2).to_broadcast(wide), ALU.subtract)\
                    .then_inc(s["logits_shifted"], 1)

            def route_softmax(b):
                dve.wait_ge(s["gates_exped"], b + 1)
                step(v.tensor_reduce(route_sum[:, :], gates[:, :, :], AX.X, ALU.add))
                step(v.reciprocal(route_inv[:, :], route_sum[:, :]))
                step(v.tensor_tensor(gates[:, :, :], gates[:, :, :], route_inv[:, :].unsqueeze(2).to_broadcast(wide), ALU.mult))

            def compare_gates():
                for t in range(NT):
                    last = v.max(top8[:, t, :], gates[:, t, :])
                step(last)
                kth = top8[:, :, TOPK - 1:TOPK].to_broadcast(wide)
                v.tensor_tensor(above[:, :, :], gates[:, :, :], kth, ALU.is_gt)
                step(v.tensor_tensor(ties[:, :, :], gates[:, :, :], kth, ALU.is_equal))
                v.tensor_reduce(n_above[:, :], above[:, :, :], AX.X, ALU.add).then_inc(s["ties_ready"], 1)

            def choose_experts(b):
                dve.wait_ge(s["ties_masked"], b + 1)
                step(v.tensor_reduce(rank[:, :, :], tied[:, :, :, :], AX.X, ALU.add))
                step(v.tensor_tensor(rank[:, :, :], rank[:, :, :], n_above[:, :].unsqueeze(2).to_broadcast(wide), ALU.add))
                step(v.scalar_tensor_tensor(ties[:, :, :], rank[:, :, :], float(TOPK), ties[:, :, :], ALU.is_lt, ALU.mult))
                step(v.tensor_tensor(ties[:, :, :], ties[:, :, :], above[:, :, :], ALU.add))
                v.tensor_tensor(cw[:, :, 0:E], ties[:, :, :], gates[:, :, :], ALU.mult).then_inc(s["cw_ready"], 1)

            def experts(b):
                dve.wait_ge(s["bias_made"], b + 1)
                v.tensor_copy(ffn[:, :, :], b_pt[1][:, :].rearrange("p (t n) -> p t n", t=NT)).then_inc(s["ffn_init"], 1)
                dve.wait_ge(s["ffn_init"], b + 1)
                for e in range(EA):
                    dve.wait_ge(s["ye_made"], EA * b + e + 1)
                    if e:
                        dve.wait_ge(s["ye_added"], EA * b + e)
                    for t in range(NT):
                        last = v.scalar_tensor_tensor(ffn[:, t, :], b_pt[e % 2][:, t * P:(t + 1) * P], cw[:, t, e:e + 1],
                                                      ffn[:, t, :], ALU.mult, ALU.add)
                    last.then_inc(s["ye_added"], 1)
                dve.wait_ge(s["ye_added"], EA * b + EA)

            def finish(b, n):
                normalise(n, normed, ffn_tiles).then_inc(s["normed_made"], 1)
                dve.wait_ge(s["normed_made"], 2 * b + 2)
                dve.wait_ge(s["stored"], 16 * b + 16)
                v.tensor_tensor(result[:, :, :], normed[:, :, :], x1[:, :, :], ALU.add).then_inc(s["result_ready"], 1)

            def move_attention(b):
                dve.wait_ge(s["att_made"], b + 1)
                v.tensor_copy(att_t[:, :], b_att[:, :]).then_inc(s["att_moved"], 1)

            def add_attention(b, n):
                normalise(n, normed, att_tiles).then_inc(s["normed_made"], 1)
                dve.wait_ge(s["res_loaded"], 16 * b + 16)
                dve.wait_ge(s["normed_made"], 2 * b + 1)
                v.tensor_tensor(x1[:, :, :], normed[:, :, :], x_res[:, :, :], ALU.add).then_inc(s["x1_ready"], 1)

            att_tiles = [b_pt[0][:, t * P:(t + 1) * P] for t in range(NT)]
            x1_tiles = [x1[:, t, :] for t in range(NT)]
            ffn_tiles = [ffn[:, t, :] for t in range(NT)]
            for k in range(1, 8, 2):
                move_values(k, k + 1)
            q_low(1)
            lookahead(1)
            silu(1, 0)
            for h in range(FFN_HEAD + 1):
                head(0, h)

            with dve.Fori(0, B - 1) as b:
                for h in range(FFN_HEAD + 1, H):
                    head(b, h)
                v0 = 16 * b + 17
                move_values(1, v0 + 1)
                move_values(3, v0 + 3)
                move_attention(b)
                move_values(5, v0 + 5)
                q_low(H * b + H + 1)
                lookahead(H * b + H + 1)
                move_values(7, v0 + 7)
                silu(H * b + H + 1, 0)
                dve.wait_ge(s["atok_made"], b + 1)
                norm_stats(att_tiles)
                add_attention(b, 4 * b + 3)
                for h in range(FFN_HEAD):
                    head(b + 1, h, finishing=b)
                experts(b)
                head(b + 1, FFN_HEAD, finished=b)
            for h in range(FFN_HEAD + 1, H):
                head(B - 1, h)
            last_b = B - 1
            move_attention(last_b)
            dve.wait_ge(s["atok_made"], last_b + 1)
            norm_stats(att_tiles)
            add_attention(last_b, 4 * last_b + 2)
            dve.wait_ge(s["x1_ready"], last_b + 1)
            norm_stats(x1_tiles)
            normalise(4 * last_b + 3, x1n, x1_tiles).then_inc(s["x1n_ready"], 1)
            x1n_low(last_b, b_u)
            shift_logits(last_b)
            route_softmax(last_b)
            compare_gates()
            choose_experts(last_b)
            experts(last_b)
            norm_stats(ffn_tiles)
            finish(last_b, 4 * last_b + 4)


_INS = ["x", "w_qkv", "w_out", "router_W", "router_b", "sW1", "sb1", "sW2", "sb2", "eW1", "eb1", "eW2", "eb2"]


def kernel(**inputs):
    import numpy as np
    import concourse.bacc as bacc
    from concourse.bass_utils import run_bass_kernel_spmd

    nc = bacc.Bacc("TRN2", target_bir_lowering=False, num_devices=1)
    arrays, args = {}, []
    for n in _INS:
        a = np.ascontiguousarray(inputs[("L0_attn_" if n in _INS[:3] else "L0_ffn_") + n])
        arrays[f"in_{n}"] = a
        args.append(nc.dram_tensor(f"in_{n}", a.shape, F32, kind="ExternalInput").ap())
    args.append(nc.dram_tensor("out", (B, S, D), F32, kind="ExternalOutput").ap())
    castle_moe(nc, *args)
    return run_bass_kernel_spmd(nc, [arrays], core_ids=[0]).results[0]["out"]
```

```python
import concourse.bass as bass
from concourse import mybir
from contextlib import ExitStack

P = 128
B, S, D = 8, 512, 128
H = 8
NT = S // P
E = 15
EA = E + 1
TOPK = 3
SCALE = float(D) ** -0.5
EPS = 1e-5
MASKED = -1e30
BIG = 3e38
F32 = mybir.dt.float32
F32R = mybir.dt.float32r
FFN_HEAD = 4
LOOP_HEAD = 6
P_GROUPS = [3], [2], [1, 0]
ROWS = [3, 2, 1, 0]
QKVS = dict(qu=0, ku=1, vu=2, q=3, k=4, v=5)


def castle_moe(nc, x, w_qkv, w_out, router_w, router_b, s_w1, s_b1, s_w2, s_b2, e_w1, e_b1, e_w2, e_b2, out):
    ALU, ACT, AX = mybir.AluOpType, mybir.ActivationFunctionType, mybir.AxisListType
    ctx = ExitStack()
    with ctx:
        def sb(name, shape, dt=F32):
            return ctx.enter_context(nc.sbuf_tensor(name, shape, dt))

        def sem(name):
            return ctx.enter_context(nc.semaphore(name))

        vu = sb("vu", [P, NT, H * D])
        vp_hi, vp_lo = sb("vp_hi", [P, NT - 1, H * D], F32R), sb("vp_lo", [P, NT - 1, H * D], F32R)
        PROBS, VP_LAST, P_LAST, NEG_SILU, LA, TANH, WORK = 0, 1280, 2304, 2560, 6144, 6656, 7168
        work = sb("work", [P, WORK])
        w_t = work[:, 0:5 * 1024].rearrange("p (m n) -> p m n", m=5)
        w_raw = dict(vu=work[:, 5 * 1024:6 * 1024], qu=work[:, 6 * 1024:7 * 1024],
                     **{n: vu[:, t, :] for t, n in enumerate(["ku", "q", "k", "v"])})
        row_start = [P * (i * (i + 1) // 2) for i in range(NT)]
        probs = [work[:, PROBS + row_start[i]:PROBS + row_start[i] + (i + 1) * P] for i in range(NT)]
        vp_last = work[:, VP_LAST:P_LAST]
        p_last = [work[:, P_LAST + n * P:P_LAST + (n + 1) * P] for n in range(2)]
        p_hi = [sb(f"p_hi{n}", [P, 10 * P], F32R) for n in range(2)]
        p_lo = [sb(f"p_lo{n}", [P, 10 * P], F32R) for n in range(2)]
        SILU_ROW = (NT - 1) * P
        SILU_SIZE = (NT - 1) * S + P
        neg_silu_all = work[:, NEG_SILU:NEG_SILU + 2 * SILU_SIZE]
        neg_silu = [[neg_silu_all[:, n * SILU_SIZE + i * SILU_ROW:n * SILU_SIZE + i * SILU_ROW + (i + 1) * P]
                     for i in range(NT)] for n in range(2)]
        diag = [work[:, NEG_SILU + n * SILU_SIZE:NEG_SILU + n * SILU_SIZE + NT * S].rearrange("p (i j) -> p i j", j=S)[:, :, 0:P]
                for n in range(2)]
        la_t = work[:, LA:TANH].rearrange("p (t q) -> p t q", t=NT)
        tanh_su = work[:, TANH:WORK].rearrange("p (t q) -> p t q", t=NT)
        late = sb("late", [P, 3072])
        w1_raw = late[:, 0:2048].rearrange("p (e n) -> p e n", e=EA)
        wo_raw = late[:, 2048:3072].rearrange("p (h n) -> p h n", h=H)
        hidden = [late[:, n * 512:(n + 1) * 512] for n in range(2)]
        ffn, result, normed, x1 = (late[:, n * 512:(n + 1) * 512].rearrange("p (t n) -> p t n", t=NT) for n in range(2, 6))
        mq_hi, mq_lo = sb("mq_hi", [P, H * D], F32R), sb("mq_lo", [P, H * D], F32R)
        mu_hi, mu_lo = sb("mu_hi", [P, H * D], F32R), sb("mu_lo", [P, H * D], F32R)
        wv_hi, wv_lo = sb("wv_hi", [P, H * D], F32R), sb("wv_lo", [P, H * D], F32R)
        wu_hi, wu_lo = sb("wu_hi", [P, H * D], F32R), sb("wu_lo", [P, H * D], F32R)
        w1_hi, w1_lo = sb("w1_hi", [P, EA, D], F32R), sb("w1_lo", [P, EA, D], F32R)
        w2 = sb("w2", [P, EA, D])
        b1_raw, b1 = sb("b1_raw", [EA, D]), sb("b1", [P, EA])
        b2 = sb("b2", [EA, D])
        rw, rb = sb("rw", [P, E]), sb("rb", [P, E])
        ident, quarter = sb("ident", [P, P]), sb("quarter", [P, NT, P])
        lower = sb("lower", [P, E, E])
        half_power = sb("half_power", [P, NT])
        x_in, x_res = sb("x_in", [P, NT, D]), sb("x_res", [P, NT, D])
        xn = sb("xn", [P, NT, D])
        xn_t, xn_hi, xn_lo = sb("xn_t", [P, S]), sb("xn_hi", [P, S], F32R), sb("xn_lo", [P, S], F32R)
        q_hi, q_lo, qu_t = sb("q_hi", [P, S], F32R), sb("q_lo", [P, S], F32R), sb("qu_t", [P, S])
        neg_max, row_sum, row_inv = sb("neg_max", [P, NT]), sb("row_sum", [P, NT]), sb("row_inv", [P, NT])
        att_t = sb("att_t", [P, S])
        stats, mv = sb("stats", [P, NT, 6]), sb("mv", [P, NT, 2])
        var_eps, rstd = sb("var_eps", [P, NT]), sb("rstd", [P, NT])
        x1n = sb("x1n", [P, NT, D])
        y_t, y_hi, y_lo = sb("y_t", [P, S]), sb("y_hi", [P, S], F32R), sb("y_lo", [P, S], F32R)
        top, route_sum, route_inv = sb("top", [P, NT]), sb("route_sum", [P, NT]), sb("route_inv", [P, NT])
        logits, gates = sb("logits", [P, NT, E]), sb("gates", [P, NT, E])
        above, ties, rank = sb("above", [P, NT, E]), sb("ties", [P, NT, E]), sb("rank", [P, NT, E])
        tied, top8, n_above = sb("tied", [P, NT, E, E]), sb("top8", [P, NT, 8]), sb("n_above", [P, NT])
        cw, cw_t = sb("cw", [P, NT, EA]), sb("cw_t", [EA, S])

        bank = [ctx.enter_context(nc.psum_tensor(f"bank{n}", [P, 512], F32)) for n in range(8)]
        b_att, b_q, b_u, b_la = bank[0], bank[1], bank[2], bank[3]
        b_rows, b_pt = bank[4:6], bank[6:8]

        VALUES_V = [1, 3, 8, 9, 10, 11, 12, 13]
        VALUES_A = [0, 2, 4, 5, 6, 7, 14, 15]
        VALUE_BANK = [5, 4, 7, 5, 4, 7, 5, 4, 7, 0, 4, 5, 1, 7, 6, 0]

        YE_BANK = [bank[6], bank[7], bank[3], bank[1]]
        CW_BEFORE, BIAS_BEFORE = 3, 5
        b_cw = bank[2]

        def value_bank(k):
            return bank[VALUE_BANK[k]]

        names = """wo_loaded x_loaded ffn_loaded res_loaded consts_made stored
            wt_made wt_moved_a wt_moved_v prod_made prod_hi prod_lo wu_hi_made w1_hi_made w1_lo_made splits_made silu_zeroed b1_made b1_moved
            xn_ready xt_made xt_moved xhi_made xlo_made x1_ready val_made val_hi val_moved_a val_moved_v
            q_made u_made qhi_made qlo_made u_moved quku_made tanh_la la_made su_made tanh_made silu_made silu_masked
            row_made row_maxed row_exped inv_made row_normed pt_made pt_hi pt_moved att_made att_moved atok_made
            stats_made mv_made var_ready rstd_ready x1n_ready normed_made yt_made yt_moved yhi_made ylo_made
            logits_made logits_moved logits_shifted gates_exped route_step ties_ready ties_masked cw_ready cwt_made cwt_moved bias_made bias_added
            hid_made hid_ready ye_made ye_added result_ready""".split()
        s = {n: sem(n) for n in names}
        for n in QKVS:
            s["w_" + n] = sem("w_" + n)

        def p_blocks(dst, src, rows):
            at = 0
            for i in rows:
                n = min(i + 1, NT - 1)
                yield (dst[:, i * P:i * P + 9 * P].rearrange("p (j q) -> p j q", j=3)[:, 0:n, 0:P] if i <= 1 else
                       dst[:, P:10 * P].rearrange("p (j q) -> p j q", j=3)[:, 0:n, (i - 1) * P:i * P],
                       src[:, at:at + n * P].rearrange("p (j q) -> p j q", q=P))
                at += (i + 1) * P

        def p_bank(h, n):
            return (b_pt[0], b_pt[1], b_u if h >= H - 2 else b_q)[n]

        def normalise(dst, tiles, which=range(NT)):
            for t in which:
                last = nc.vector.tensor_scalar(dst[:, t, :], tiles[t], mv[:, t, 0:1], rstd[:, t:t + 1], ALU.subtract, ALU.mult)
            return last

        x_tiles = [x_in[:, t, :] for t in range(NT)]
        att_tiles = [b_pt[0][:, t * P:(t + 1) * P] for t in range(NT)]
        x1_tiles = [x1[:, t, :] for t in range(NT)]
        ffn_tiles = [ffn[:, t, :] for t in range(NT)]

        block = ctx.enter_context(nc.Block())
        xv = x.rearrange("b (t p) d -> b p t d", p=P)
        ov = out.rearrange("b (t p) d -> b p t d", p=P)
        order = ["qu", "ku", "q", "k", "v"]
        PRODUCT_BANK = [2, 3, 0, 6, 7, 1]
        products = [("mu", 0, 1), ("mq", 2, 3), ("wv", 4, None)]
        prod_dst = dict(mu=(mu_hi, mu_lo), mq=(mq_hi, mq_lo), wv=(wv_hi, wv_lo))

        @block.sync
        def _(sp):
            for n in order[0:2] + ["vu"] + order[2:]:
                if n == order[1]:
                    sp.dma_start(x_in[:, :, :], xv[0]).then_inc(s["x_loaded"], 16)
                sp.dma_start(w_raw[n], w_qkv[:, QKVS[n] * 1024:(QKVS[n] + 1) * 1024]).then_inc(s["w_" + n], 16)
            sp.dma_start(wo_raw[:, :, :], w_out.rearrange("(h p) n -> p h n", p=P)).then_inc(s["wo_loaded"], 16)
            sp.dma_start(w1_raw[:, 0:E, :], e_w1.rearrange("e d n -> d e n")).then_inc(s["ffn_loaded"], 16)
            sp.dma_start(w1_raw[:, E, :], s_w1).then_inc(s["ffn_loaded"], 16)
            sp.dma_start(w2[:, 0:E, :], e_w2.rearrange("e d n -> d e n")).then_inc(s["ffn_loaded"], 16)
            sp.dma_start(w2[:, E, :], s_w2).then_inc(s["ffn_loaded"], 16)
            sp.dma_start(b1_raw[0:E, :], e_b1).then_inc(s["ffn_loaded"], 16)
            sp.dma_start(b1_raw[E:EA, :], s_b1.rearrange("(a n) -> a n", a=1)).then_inc(s["ffn_loaded"], 16)
            sp.dma_start(b2[0:E, :], e_b2).then_inc(s["ffn_loaded"], 16)
            sp.dma_start(b2[E:EA, :], s_b2.rearrange("(a n) -> a n", a=1)).then_inc(s["ffn_loaded"], 16)
            sp.dma_start(rw[:, :], router_w).then_inc(s["ffn_loaded"], 16)
            sp.dma_start(rb[:, :], router_b.partition_broadcast(P)).then_inc(s["stored"], 16)

            def load_x(b):
                sp.wait_ge(s["xn_ready"], b)
                sp.dma_start(x_in[:, :, :], xv[b]).then_inc(s["x_loaded"], 16)

            def load_residual(b):
                sp.wait_ge(s["x1_ready"], b)
                sp.dma_start(x_res[:, :, :], xv[b]).then_inc(s["res_loaded"], 16)

            def store(b):
                sp.wait_ge(s["result_ready"], b + 1)
                sp.dma_start(ov[b], result[:, :, :]).then_inc(s["stored"], 16)

            load_x(1)
            sp.dma_start(x_res[:, :, :], xv[0]).then_inc(s["res_loaded"], 16)
            with sp.Fori(0, B - 2) as b:
                load_x(b + 2)
                load_residual(b + 1)
                store(b)
            load_residual(B - 1)
            store(B - 2)
            store(B - 1)
            sp.wait_ge(s["stored"], 16 * (B + 1))

        @block.gpsimd
        def _(pool):
            g = nc.gpsimd
            silu_count, row_count = pool.alloc_register("silu_count"), pool.alloc_register("row_count")
            pool.reg_mov(silu_count, 0)
            pool.reg_mov(row_count, 0)
            g.memset(ident[:, :], 0.0).then_inc(s["consts_made"], 1)
            g.memset(quarter[:, :, :], 0.25).then_inc(s["consts_made"], 1)
            g.memset(lower[:, :, :], 1.0).then_inc(s["consts_made"], 1)
            g.memset(half_power[:, :], -0.5).then_inc(s["consts_made"], 1)
            g.memset(cw[:, :, E:EA], 1.0).then_inc(s["consts_made"], 1)
            pool.wait_ge(s["consts_made"], 5)
            g.affine_select(out=ident[:, :], in_=ident[:, :], compare_op=ALU.not_equal, fill=1.0, base=0,
                            pattern=[[-1, P]], channel_multiplier=1).then_inc(s["consts_made"], 1)
            g.affine_select(out=quarter[:, :, :], in_=quarter[:, :, :], compare_op=ALU.is_gt, fill=0.0, base=0,
                            pattern=[[0, NT], [-1, P]], channel_multiplier=1).then_inc(s["consts_made"], 1)
            g.affine_select(out=lower[:, :, :], in_=lower[:, :, :], compare_op=ALU.is_gt, fill=0.0, base=0,
                            pattern=[[1, E], [-1, E]], channel_multiplier=0).then_inc(s["consts_made"], 1)

            def inv_sqrt(n):
                pool.wait_ge(s["var_ready"], n)
                g.tensor_tensor(rstd[:, :], var_eps[:, :], half_power[:, :], ALU.pow).then_inc(s["rstd_ready"], 1)

            def whole(dst, hi, lo):
                return g.tensor_tensor(dst, hi.bitcast(F32), lo.bitcast(F32), ALU.add)

            def whole_x(n):
                pool.wait_ge(s["xlo_made"], n)
                whole(xn_t[:, :], xn_hi[:, :], xn_lo[:, :]).then_inc(s["xt_moved"], 1)

            def whole_y(b):
                pool.wait_ge(s["ylo_made"], b + 1)
                whole(y_t[:, :], y_hi[:, :], y_lo[:, :]).then_inc(s["yt_moved"], 1)

            def finish(b):
                pool.wait_ge(s["stored"], 16 * b + 16)
                pool.wait_ge(s["normed_made"], 2 * b + 2)
                g.tensor_tensor(result[:, :, :], normed[:, :, :], x1[:, :, :], ALU.add).then_inc(s["result_ready"], 1)

            def add_attention(b):
                pool.wait_ge(s["res_loaded"], 16 * b + 16)
                pool.wait_ge(s["normed_made"], 2 * b + 1)
                g.tensor_tensor(x1[:, :, :], normed[:, :, :], x_res[:, :, :], ALU.add).then_inc(s["x1_ready"], 1)

            def mask_silu(h):
                pool.reg_add(silu_count, silu_count, 1)
                pool.wait_ge(s["consts_made"], 8)
                pool.wait_ge(s["silu_made"], silu_count)
                g.affine_select(out=diag[h % 2], in_=diag[h % 2], compare_op=ALU.is_ge, fill=MASKED, base=0,
                                pattern=[[0, NT], [-1, P]], channel_multiplier=1).then_inc(s["silu_masked"], 1)

            def head(b, h, masks=True, norm=None, routing=None):
                for n, i in enumerate(ROWS):
                    if n == 2 and routing is not None:
                        mask_ties(routing)
                    pool.reg_add(row_count, row_count, 1)
                    pool.wait_ge(s["consts_made"], 8)
                    pool.wait_ge(s["inv_made"], row_count)
                    g.tensor_scalar(probs[i], probs[i], row_inv[:, i:i + 1], 1.0,
                                    ALU.mult, ALU.mult).then_inc(s["row_normed"], 1)
                if norm is not None:
                    inv_sqrt(norm)
                if masks:
                    mask_silu(h + 1)

            def mask_ties(b):
                pool.wait_ge(s["ties_ready"], b + 1)
                pairs = [P, NT, E, E]
                g.tensor_tensor(tied[:, :, :, :], ties[:, :, :].unsqueeze(2).to_broadcast(pairs),
                                lower[:, :, :].unsqueeze(1).to_broadcast(pairs), ALU.mult).then_inc(s["ties_masked"], 1)

            inv_sqrt(1)
            whole_x(1)
            pool.wait_ge(s["prod_made"], 6)
            g.memset(neg_silu_all, 0.0).then_inc(s["silu_zeroed"], 1)
            mask_silu(0)
            for h in range(LOOP_HEAD):
                head(0, h)
                if h < 2:
                    pool.wait_ge(s["w1_hi_made"], 1)
                    e = slice(h * EA // 2, (h + 1) * EA // 2)
                    g.tensor_tensor(w1_lo[:, e, :], w1_raw[:, e, :], w1_hi[:, e, :].bitcast(F32), ALU.subtract)\
                        .then_inc(s["w1_lo_made"], 1)
            with pool.Fori(0, B - 1) as b:
                for h in range(LOOP_HEAD, H):
                    head(b, h, masks=h < H - 1, norm=4 * b + 2 if h == H - 2 else None)
                whole_x(b + 2)
                inv_sqrt(4 * b + 3)
                mask_silu(0)
                add_attention(b)
                for h in range(LOOP_HEAD):
                    head(b + 1, h, norm={0: 4 * b + 4, FFN_HEAD: 4 * b + 5}.get(h), routing=b if h == 3 else None)
                    if h == 1:
                        whole_y(b)
                    if h == FFN_HEAD + 1:
                        finish(b)
            for h in range(LOOP_HEAD, H):
                head(B - 1, h, masks=h < H - 1)
            inv_sqrt(4 * B - 2)
            inv_sqrt(4 * B - 1)
            mask_ties(B - 1)
            inv_sqrt(4 * B)

        @block.tensor
        def _(pe):
            mm = nc.tensor.matmul

            def mm3(dst, a_hi, a_lo, c_hi, c_lo, start=True, stop=True, skip=False):
                mm(dst, a_lo, c_hi, start=start, stop=False, skip_group_check=skip)
                mm(dst, a_hi, c_lo, start=False, stop=False, skip_group_check=skip)
                return mm(dst, a_hi, c_hi, start=False, stop=stop, skip_group_check=skip)

            def tile(t):
                return slice(t * P, (t + 1) * P)

            def transpose_x():
                for t in range(NT):
                    last = nc.tensor.transpose(b_q[:, tile(t)], xn[:, t, :], ident[:, :])
                last.then_inc(s["xt_made"], 1)

            def value_group(k, b):
                before = [n for n in range(k) if VALUE_BANK[n] == VALUE_BANK[k]]
                if before:
                    wait_values(before[-1], b)
                elif VALUE_BANK[k] == 1:
                    pe.wait_ge(s["qlo_made"], H * b + 1)
                if k == 14:
                    pe.wait_ge(s["b1_moved"], 1)
                    if not isinstance(b, int):
                        pe.wait_ge(s["normed_made"], 2 * b - 1)
                hi, lo = ((wu_hi, wu_lo), (wv_hi, wv_lo))[k // 8]
                t, half = (k % 8) // 2, k % 2
                c = slice(half * 512, half * 512 + 512)
                mm3(value_bank(k)[:, :], xn_hi[:, tile(t)], xn_lo[:, tile(t)], hi[:, c], lo[:, c])\
                    .then_inc(s["val_made"], 1)

            def wait_values(k, b):
                if k in VALUES_V:
                    pe.wait_ge(s["val_moved_v"], len(VALUES_V) * b + VALUES_V.index(k) + 1)
                else:
                    pe.wait_ge(s["val_moved_a"], len(VALUES_A) * b + VALUES_A.index(k) + 1)

            def project_u(h):
                c = slice(h * D, (h + 1) * D)
                mm3(b_u[:, :], mu_hi[:, c], mu_lo[:, c], xn_hi[:, :], xn_lo[:, :]).then_inc(s["u_made"], 1)

            def project_q(h):
                c = slice(h * D, (h + 1) * D)
                mm3(b_q[:, :], mq_hi[:, c], mq_lo[:, c], xn_hi[:, :], xn_lo[:, :]).then_inc(s["q_made"], 1)

            def lookahead_logits(g1, first_of=None):
                pe.wait_ge(s["u_moved"], g1)
                if first_of is not None:
                    pe.wait_ge(s["xt_moved"], first_of + 1)
                if not isinstance(g1, int) or g1 > 1:
                    pe.wait_ge(s["silu_made"], g1 - 1)
                for t in range(NT):
                    last = mm(b_la[:, tile(t)], xn_t[:, tile(t)], qu_t[:, tile(t)], start=True, stop=True)
                last.then_inc(s["quku_made"], 1)

            def lookahead_sum(h, g1):
                pe.wait_ge(s["la_made"], g1)
                for t in range(NT):
                    last = mm(b_la[:, tile(t)], la_t[:, t, :], vu[:, t, h * D:(h + 1) * D], start=True, stop=True)
                last.then_inc(s["su_made"], 1)

            def score_row(n):
                i = ROWS[n]
                w = (i + 1) * P
                mm3(b_rows[n % 2][:, 0:w], q_hi[:, tile(i)], q_lo[:, tile(i)], xn_hi[:, 0:w], xn_lo[:, 0:w])\
                    .then_inc(s["row_made"], 1)

            def transpose_rows(rows, dst):
                at = 0
                for i in rows:
                    for j in range(i + 1):
                        last = nc.tensor.transpose(dst[:, at:at + P], probs[i][:, tile(j)], ident[:, :])
                        at += P
                last.then_inc(s["pt_made"], 1)

            def attend(h, j, first=False, end=False):
                c = slice(h * D, (h + 1) * D)
                if j == NT - 1:
                    return mm(b_att[:, j * P:S], vp_last[:, c], p_last[h % 2], start=first, stop=end, skip_group_check=True)
                at = slice(4 * j * P, (3 * j + NT) * P)
                return mm3(b_att[:, j * P:S], vp_hi[:, j, c], vp_lo[:, j, c], p_hi[h % 2][:, at], p_lo[h % 2][:, at],
                           start=first, stop=end, skip=True)

            def hidden_layer(e):
                mm3(b_rows[e % 2][:, :], w1_hi[:, e, :], w1_lo[:, e, :], y_hi[:, :], y_lo[:, :]).then_inc(s["hid_made"], 1)

            def output_layer(b, e):
                pe.wait_ge(s["hid_ready"], EA * b + e + 1)
                if e < 4 and not isinstance(b, int):
                    if e == 2:
                        pe.wait_ge(s["silu_made"], H * b + H + FFN_HEAD + 1)
                    else:
                        pe.wait_ge(s["pt_moved"], 3 * (H * b + H + FFN_HEAD) - {0: 2, 1: 1, 3: 0}[e])
                if e >= 4:
                    pe.wait_ge(s["ye_added"], EA * b + e - 3)
                for t in range(NT):
                    last = mm(YE_BANK[e % 4][:, tile(t)], hidden[e % 2][:, tile(t)], w2[:, e, :], start=True, stop=True)
                last.then_inc(s["ye_made"], 1)

            pe.wait_ge(s["consts_made"], 8)
            for k in range(10):
                m, half = k // 2, k % 2
                if half == 0:
                    pe.wait_ge(s["w_" + order[m]], 16)
                if k >= 4:
                    pe.wait_ge(s["wt_moved_a" if k % 2 == 0 else "wt_moved_v"], (k - 4) // 2 + 1)
                for n in range(4):
                    c = (half * 4 + n) * D
                    last = nc.tensor.transpose(bank[4 + k % 4][:, tile(n)], w_raw[order[m]][:, c:c + D], ident[:, :])
                last.then_inc(s["wt_made"], 1)
                if k == 3:
                    pe.wait_ge(s["xn_ready"], 1)
                    transpose_x()
            k = 0
            for name, left, right in products:
                moved = (left if right is None else right) + 1
                pe.wait_ge(s["wt_moved_a"], moved)
                pe.wait_ge(s["wt_moved_v"], moved)
                if right is None:
                    pe.wait_ge(s["wo_loaded"], 16)
                    pe.wait_ge(s["xlo_made"], 1)
                for half in range(2):
                    for n in range(4):
                        h = half * 4 + n
                        rhs = wo_raw[:, h, :] if right is None else w_t[:, right, h * D:(h + 1) * D]
                        last = mm(bank[PRODUCT_BANK[k]][:, tile(n)], w_t[:, left, h * D:(h + 1) * D], rhs, start=True, stop=True)
                    last.then_inc(s["prod_made"], 1)
                    k += 1

            def head(b, h, finishing=None, finished=None):
                g0 = H * b + h
                if not (finished is not None and h == FFN_HEAD):
                    pe.wait_ge(s["qlo_made"], g0 + 1)
                    if h == 0:
                        wait_values(10, b)
                    score_row(0)
                if h == 0:
                    wait_values(11, b)
                score_row(1)
                if finished is not None and h == FFN_HEAD:
                    pe.wait_ge(s["ye_added"], EA * finished + EA - 1)
                if h < H - 1:
                    lookahead_logits(g0 + 2)
                if h >= 2:
                    pe.wait_ge(s["pt_moved"], 3 * g0 - 1)
                    attend(h - 1, 2)
                    attend(h - 1, 3)
                if finishing is not None and h == 2:
                    router_logits(finishing, b_u)
                pe.wait_ge(s["row_maxed"], 4 * g0 + 1)
                score_row(2)
                pe.wait_ge(s["row_maxed"], 4 * g0 + 2)
                score_row(3)
                if h == 0:
                    value_group(14, b)
                    value_group(15, b)
                if h == 1:
                    wait_values(15, b)
                if h:
                    pe.wait_ge(s["pt_moved"], 3 * g0)
                    attend(h - 1, 0, first=h == 1)
                if h == H - 1 and not isinstance(b, int):
                    pe.wait_ge(s["xn_ready"], b + 2)
                    transpose_x()
                if finishing is not None and h == 1:
                    transpose_x1n(finishing, b_u)
                if h < H - 1:
                    lookahead_sum(h + 1, g0 + 2)
                    project_q(h + 1)
                if finishing is not None and h == 2:
                    pe.wait_ge(s["logits_moved"], finishing + 1)
                pe.wait_ge(s["row_normed"], 4 * g0 + 1)
                if h == 0:
                    wait_values(14, b)
                transpose_rows(P_GROUPS[0], b_pt[0])
                if h and h < H - 1:
                    attend(h - 1, 1)
                pe.wait_ge(s["row_normed"], 4 * g0 + 2)
                if h == 0:
                    wait_values(13, b)
                transpose_rows(P_GROUPS[1], b_pt[1])
                if h < H - 2 and not (finishing is not None and h == 1):
                    project_u(h + 2)
                if h == 1:
                    attend(h - 1, 2)
                    attend(h - 1, 3)
                if finishing is not None and h == 1:
                    pe.wait_ge(s["ylo_made"], finishing + 1)
                    project_u(h + 2)
                if h == H - 1:
                    attend(h - 1, 1)
                if h < H - 2:
                    pe.wait_ge(s["qlo_made"], g0 + 2)
                if finishing is not None and h == FFN_HEAD - 1:
                    hidden_layer(0)
                pe.wait_ge(s["row_normed"], 4 * g0 + 4)
                transpose_rows(P_GROUPS[2], p_bank(h, 2))

            def transpose_x1n(b, dst):
                pe.wait_ge(s["x1n_ready"], b + 1)
                for t in range(NT):
                    last = nc.tensor.transpose(dst[:, tile(t)], x1n[:, t, :], ident[:, :])
                last.then_inc(s["yt_made"], 1)

            def router_logits(b, dst):
                pe.wait_ge(s["yt_moved"], b + 1)
                for t in range(NT):
                    c = slice(t * 16, t * 16 + E)
                    last = mm(dst[:, c], y_t[:, tile(t)], rw[:, :], start=True, stop=True)
                last.then_inc(s["logits_made"], 1)

            def transpose_gates(b):
                pe.wait_ge(s["cw_ready"], b + 1)
                if not isinstance(b, int):
                    pe.wait_ge(s["u_moved"], H * b + H + FFN_HEAD + 2)
                for t in range(NT):
                    last = nc.tensor.transpose(b_cw[0:EA, tile(t)], cw[:, t, :], ident[:, :])
                last.then_inc(s["cwt_made"], 1)

            def gated_biases(b):
                pe.wait_ge(s["cwt_moved"], b + 1)
                for t in range(NT):
                    last = mm(b_cw[:, tile(t)], cw_t[:, tile(t)], b2[:, :], start=True, stop=True)
                last.then_inc(s["bias_made"], 1)

            def experts(b):
                if isinstance(b, int):
                    pe.wait_ge(s["ylo_made"], b + 1)
                    hidden_layer(0)
                hidden_layer(1)
                for e in range(EA):
                    if e == CW_BEFORE:
                        transpose_gates(b)
                    if e == BIAS_BEFORE:
                        gated_biases(b)
                    if e == EA - 1 and not isinstance(b, int):
                        pe.wait_ge(s["qlo_made"], H * b + H + FFN_HEAD + 1)
                        score_row(0)
                    output_layer(b, e)
                    if e + 2 < EA:
                        hidden_layer(e + 2)

            def attend_last(b):
                pe.wait_ge(s["pt_moved"], 3 * (H * b + H) - 1)
                attend(H - 1, 2)
                attend(H - 1, 3)
                pe.wait_ge(s["pt_moved"], 3 * (H * b + H))
                attend(H - 1, 0)
                attend(H - 1, 1, end=True).then_inc(s["att_made"], 1)

            def attention_tokens(b):
                pe.wait_ge(s["att_moved"], b + 1)
                for t in range(NT):
                    last = nc.tensor.transpose(b_pt[0][:, tile(t)], att_t[:, tile(t)], ident[:, :])
                last.then_inc(s["atok_made"], 1)

            pe.wait_ge(s["splits_made"], 1)
            value_group(0, 0)
            value_group(1, 0)
            pe.wait_ge(s["prod_lo"], 6)
            for k in range(2, 8):
                value_group(k, 0)
            project_u(0)
            project_q(0)
            lookahead_logits(1, first_of=0)
            for k in range(8, 12):
                value_group(k, 0)
            wait_values(3, 0)
            wait_values(7, 0)
            lookahead_sum(0, 1)
            project_u(1)
            for k in range(12, 14):
                value_group(k, 0)
            pe.wait_ge(s["ffn_loaded"], 16 * 9)
            nc.tensor.transpose(b_pt[0][:, 0:EA], b1_raw[:, :], ident[0:EA, 0:EA]).then_inc(s["b1_made"], 1)
            for h in range(LOOP_HEAD):
                head(0, h)

            pe.wait_ge(s["w1_lo_made"], 2)
            pe.wait_ge(s["b1_moved"], 1)
            with pe.Fori(0, B - 1) as b:
                for h in range(LOOP_HEAD, H):
                    head(b, h)
                pe.wait_ge(s["xlo_made"], b + 2)
                value_group(0, b + 1)
                value_group(1, b + 1)
                pe.wait_ge(s["pt_moved"], 3 * (H * b + H) - 1)
                value_group(2, b + 1)
                value_group(3, b + 1)
                attend_last(b)
                project_u(0)
                value_group(4, b + 1)
                project_q(0)
                attention_tokens(b)
                value_group(5, b + 1)
                lookahead_logits(H * b + H + 1, first_of=b + 1)
                value_group(6, b + 1)
                value_group(7, b + 1)
                value_group(8, b + 1)
                value_group(9, b + 1)
                wait_values(3, b + 1)
                wait_values(7, b + 1)
                lookahead_sum(0, H * b + H + 1)
                project_u(1)
                for k in range(10, 14):
                    value_group(k, b + 1)
                for h in range(FFN_HEAD):
                    head(b + 1, h, finishing=b)
                experts(b)
                for h in range(FFN_HEAD, LOOP_HEAD):
                    head(b + 1, h, finished=b)
            for h in range(LOOP_HEAD, H):
                head(B - 1, h)
            attend_last(B - 1)
            attention_tokens(B - 1)
            transpose_x1n(B - 1, b_u)
            router_logits(B - 1, b_att)
            experts(B - 1)

        @block.scalar
        def _(act):
            a = nc.scalar.activation

            def move_x(n):
                act.wait_ge(s["xt_made"], n)
                a(xn_hi[:, :], b_q[:, :], ACT.Copy).then_inc(s["xhi_made"], 1)

            def move_values(k, made):
                act.wait_ge(s["val_made"], made)
                t, half = (k % 8) // 2, k % 2
                c = slice(half * 512, half * 512 + 512)
                if 8 <= k < 14:
                    a(vp_hi[:, t, c], value_bank(k)[:, :], ACT.Copy).then_inc(s["val_hi"], 1)
                else:
                    a(vu[:, t, c] if k < 8 else vp_last[:, c], value_bank(k)[:, :], ACT.Copy).then_inc(s["val_moved_a"], 1)

            def move_u(g1):
                act.wait_ge(s["u_made"], g1)
                a(qu_t[:, :], b_u[:, :], ACT.Copy).then_inc(s["u_moved"], 1)

            def q_high(g1):
                act.wait_ge(s["q_made"], g1)
                a(q_hi[:, :], b_q[:, :], ACT.Copy).then_inc(s["qhi_made"], 1)

            def tanh_logits(g1):
                act.wait_ge(s["quku_made"], g1)
                a(b_la[:, :], b_la[:, :], ACT.Tanh, scale=0.5).then_inc(s["tanh_la"], 1)

            def tanh_sums(g1):
                act.wait_ge(s["su_made"], g1)
                a(tanh_su[:, :, :], b_la[:, :].rearrange("p (t q) -> p t q", t=NT), ACT.Tanh, scale=-1.0)\
                    .then_inc(s["tanh_made"], 1)

            act.wait_ge(s["w_vu"], 16)
            a(wu_hi[:, :], w_raw["vu"], ACT.Copy).then_inc(s["wu_hi_made"], 1)
            for k in range(0, 10, 2):
                act.wait_ge(s["wt_made"], k + 1)
                a(w_t[:, k // 2, 0:512], bank[4 + k % 4][:, :], ACT.Copy).then_inc(s["wt_moved_a"], 1)
                if k == 2:
                    move_x(1)
            for k in range(6):
                act.wait_ge(s["prod_made"], k + 1)
                hi = prod_dst[products[k // 2][0]][0]
                a(hi[:, (k % 2) * 512:(k % 2) * 512 + 512], bank[PRODUCT_BANK[k]][:, :], ACT.Copy,
                  scale=1.0 if k >= 4 else SCALE).then_inc(s["prod_hi"], 1)

            def head(b, h, finishing=None):
                g0 = H * b + h
                for n, i in enumerate(ROWS):
                    act.wait_ge(s["row_maxed"], 4 * g0 + n + 1)
                    a(probs[i], probs[i], ACT.Exp, bias=neg_max[:, i:i + 1], scale=-1.0,
                      accum_out=row_sum[:, i:i + 1]).then_inc(s["row_exped"], 1)
                    if n == 0 and h < H - 1:
                        tanh_logits(g0 + 2)
                    if n == 1 and h == 0:
                        move_values(14, 16 * b + 15)
                if finishing is not None and h == 1:
                    move_x1n(finishing, b_u)
                if h < H - 1:
                    tanh_sums(g0 + 2)
                    q_high(g0 + 2)
                    if h == 0:
                        move_values(15, 16 * b + 16)
                elif not isinstance(b, int):
                    move_x(b + 2)
                if finishing is not None and h == 2:
                    exp_gates(finishing)
                for n, rows in enumerate(P_GROUPS):
                    if n == 2 and h < H - 2:
                        move_u(g0 + 3)
                    if n == 2 and finishing is not None and h == FFN_HEAD - 1:
                        relu(finishing, 0)
                    act.wait_ge(s["pt_made"], 3 * g0 + n + 1)
                    if 3 in rows:
                        a(p_last[h % 2], b_pt[0][:, 3 * P:4 * P], ACT.Copy)
                    for dst, src in p_blocks(p_hi[h % 2], p_bank(h, n), rows):
                        last = a(dst, src, ACT.Copy)
                    last.then_inc(s["pt_hi"], 1)

            def move_x1n(b, src):
                act.wait_ge(s["yt_made"], b + 1)
                a(y_hi[:, :], src[:, :], ACT.Copy).then_inc(s["yhi_made"], 1)

            def exp_gates(b):
                act.wait_ge(s["logits_shifted"], b + 1)
                a(gates[:, :, :], logits[:, :, :], ACT.Exp).then_inc(s["gates_exped"], 1)

            def relu(b, e):
                act.wait_ge(s["hid_made"], EA * b + e + 1)
                a(hidden[e % 2][:, :], b_rows[e % 2][:, :], ACT.Relu, bias=b1[:, e:e + 1]).then_inc(s["hid_ready"], 1)

            def experts(b):
                for e in range(0 if isinstance(b, int) else 1, EA):
                    if e == CW_BEFORE + 2:
                        act.wait_ge(s["cwt_made"], b + 1)
                        a(cw_t[:, :], b_cw[0:EA, :], ACT.Copy).then_inc(s["cwt_moved"], 1)
                    relu(b, e)

            for k in (0, 2, 4, 5, 6, 7):
                move_values(k, k + 1)
            move_u(1)
            q_high(1)
            tanh_logits(1)
            for k in range(8, 12):
                move_values(k, k + 1)
            tanh_sums(1)
            move_u(2)
            for k in range(12, 14):
                move_values(k, k + 1)
            act.wait_ge(s["b1_made"], 1)
            a(b1[:, :], b_pt[0][:, 0:EA], ACT.Copy).then_inc(s["b1_moved"], 1)
            a(w1_hi[:, :, :], w1_raw[:, :, :], ACT.Copy).then_inc(s["w1_hi_made"], 1)
            for h in range(LOOP_HEAD):
                head(0, h)

            with act.Fori(0, B - 1) as b:
                for h in range(LOOP_HEAD, H):
                    head(b, h)
                v0 = 16 * b + 17
                move_values(0, v0)
                move_values(2, v0 + 2)
                move_u(H * b + H + 1)
                move_values(4, v0 + 4)
                q_high(H * b + H + 1)
                move_values(5, v0 + 5)
                tanh_logits(H * b + H + 1)
                for k in range(6, 10):
                    move_values(k, v0 + k)
                tanh_sums(H * b + H + 1)
                move_u(H * b + H + 2)
                for k in range(10, 14):
                    move_values(k, v0 + k)
                for h in range(FFN_HEAD):
                    head(b + 1, h, finishing=b)
                experts(b)
                for h in range(FFN_HEAD, LOOP_HEAD):
                    head(b + 1, h)
            for h in range(LOOP_HEAD, H):
                head(B - 1, h)
            act.wait_ge(s["yt_made"], B)
            a(y_t[:, :], b_u[:, :], ACT.Copy).then_inc(s["yt_moved"], 1)
            move_x1n(B - 1, b_u)
            exp_gates(B - 1)
            experts(B - 1)

        @block.vector
        def _(dve):
            v = nc.vector
            norm_count, row_count = dve.alloc_register("norm_count"), dve.alloc_register("row_count")
            step_count, logit_count = dve.alloc_register("step_count"), dve.alloc_register("logit_count")
            dve.reg_mov(step_count, 0)
            dve.reg_mov(logit_count, 0)
            dve.reg_mov(norm_count, 0)
            dve.reg_mov(row_count, 0)

            def norm_stats(tiles, which=range(NT)):
                for t in which:
                    last = v.bn_stats(stats[:, t, :], tiles[t])
                if t == NT - 1:
                    last.then_inc(s["stats_made"], 1)

            def norm_aggregate():
                dve.reg_add(norm_count, norm_count, 1)
                dve.wait_ge(s["consts_made"], 8)
                dve.wait_ge(s["stats_made"], norm_count)
                for t in range(NT):
                    last = v.bn_aggr(mv[:, t, :], stats[:, t, :])
                last.then_inc(s["mv_made"], 1)
                dve.wait_ge(s["mv_made"], norm_count)
                v.tensor_scalar(var_eps[:, :], mv[:, :, 1], EPS, None, ALU.add).then_inc(s["var_ready"], 1)

            def low_part(dst, src, hi):
                return v.tensor_tensor(dst, src, hi.bitcast(F32), ALU.subtract)

            def x_low(n):
                dve.wait_ge(s["xhi_made"], n)
                low_part(xn_lo[:, :], b_q[:, :], xn_hi[:, :]).then_inc(s["xlo_made"], 1)

            def move_values(k, made):
                dve.wait_ge(s["val_made"], made)
                v.tensor_copy(vu[:, k // 2, 512:1024], value_bank(k)[:, :]).then_inc(s["val_moved_v"], 1)

            def value_low(k, b):
                dve.wait_ge(s["val_hi"], 6 * b + k - 7)
                t, half = (k % 8) // 2, k % 2
                c = slice(half * 512, half * 512 + 512)
                low_part(vp_lo[:, t, c], value_bank(k)[:, :], vp_hi[:, t, c]).then_inc(s["val_moved_v"], 1)

            def p_low(h, n, made):
                dve.wait_ge(s["pt_hi"], made)
                rows = P_GROUPS[n]
                for (dst, src), (hi, _) in zip(p_blocks(p_lo[h % 2], p_bank(h, n), rows), p_blocks(p_hi[h % 2], p_bank(h, n), rows)):
                    last = low_part(dst, src, hi)
                last.then_inc(s["pt_moved"], 1)

            def q_low(g1):
                dve.wait_ge(s["qhi_made"], g1)
                low_part(q_lo[:, :], b_q[:, :], q_hi[:, :]).then_inc(s["qlo_made"], 1)

            def lookahead(g1):
                dve.wait_ge(s["tanh_la"], g1)
                v.scalar_tensor_tensor(la_t[:, :, :], b_la[:, :].rearrange("p (t q) -> p t q", t=NT), 1.0,
                                       quarter[:, :, :], ALU.add, ALU.mult).then_inc(s["la_made"], 1)

            def silu(g1, h):
                dve.wait_ge(s["silu_zeroed"], 1)
                dve.wait_ge(s["tanh_made"], g1)
                v.scalar_tensor_tensor(diag[h % 2], tanh_su[:, :, :], 1.0, b_la[:, :].rearrange("p (t q) -> p t q", t=NT),
                                       ALU.subtract, ALU.mult).then_inc(s["silu_made"], 1)

            dve.wait_ge(s["x_loaded"], 16)
            dve.wait_ge(s["consts_made"], 8)
            norm_stats(x_tiles)
            norm_aggregate()
            dve.wait_ge(s["rstd_ready"], 1)
            normalise(xn, x_tiles).then_inc(s["xn_ready"], 1)
            for k in range(1, 10, 2):
                dve.wait_ge(s["wt_made"], k + 1)
                v.tensor_copy(w_t[:, k // 2, 512:1024], bank[4 + k % 4][:, :]).then_inc(s["wt_moved_v"], 1)
                if k == 3:
                    x_low(1)
                    dve.wait_ge(s["wu_hi_made"], 1)
                    low_part(wu_lo[:, :], w_raw["vu"], wu_hi[:, :]).then_inc(s["splits_made"], 1)
            for k in range(6):
                dve.wait_ge(s["prod_hi"], k + 1)
                hi, lo = prod_dst[products[k // 2][0]]
                c = slice((k % 2) * 512, (k % 2) * 512 + 512)
                v.scalar_tensor_tensor(lo[:, c], bank[PRODUCT_BANK[k]][:, :], 1.0 if k >= 4 else SCALE,
                                       hi[:, c].bitcast(F32), ALU.mult, ALU.subtract).then_inc(s["prod_lo"], 1)

            def max_row(n, h):
                i = ROWS[n]
                w = (i + 1) * P
                dve.reg_add(row_count, row_count, 1)
                dve.wait_ge(s["consts_made"], 8)
                dve.wait_ge(s["row_made"], row_count)
                v.tensor_tensor_reduce(out=probs[i], in0=b_rows[n % 2][:, 0:w], in1=neg_silu[h % 2][i],
                                       scale=-1.0, scalar=BIG, op0=ALU.add, op1=ALU.min,
                                       accum_out=neg_max[:, i:i + 1]).then_inc(s["row_maxed"], 1)

            def invert_sum(n, g0):
                i = ROWS[n]
                dve.wait_ge(s["row_exped"], 4 * g0 + n + 1)
                v.reciprocal(row_inv[:, i:i + 1], row_sum[:, i:i + 1]).then_inc(s["inv_made"], 1)

            def head(b, h, finishing=None, finished=None):
                g0 = H * b + h
                routing = h if finishing is not None else None
                if not (finished is not None and h == FFN_HEAD):
                    dve.wait_ge(s["silu_masked"], g0 + 1)
                    max_row(0, h)
                if routing == 3:
                    largest_gates()
                max_row(1, h)
                if routing == 3:
                    compare_gates()
                if h == 0:
                    value_low(13, b)
                if h not in (0, FFN_HEAD) or (h and isinstance(b, int)):
                    p_low(h - 1, 2, 3 * g0)
                if routing == 3:
                    count_above()
                invert_sum(0, g0)
                stat_tiles, norm, ended = None, None, None
                if finishing is not None and h == 0:
                    dve.wait_ge(s["x1_ready"], finishing + 1)
                    stat_tiles, norm = x1_tiles, (x1n, x1_tiles, 4 * finishing + 4)
                if finishing is not None and h == 1:
                    ended = x1n, x1_tiles, s["x1n_ready"]
                if finished is not None and h == FFN_HEAD:
                    dve.wait_ge(s["ye_added"], EA * finished + EA)
                    stat_tiles, norm = ffn_tiles, (normed, ffn_tiles, 4 * finished + 5)
                if finished is not None and h == FFN_HEAD + 1:
                    ended = normed, ffn_tiles, s["normed_made"]
                if h == H - 2 and not isinstance(b, int):
                    dve.wait_ge(s["x_loaded"], 16 * b + 32)
                    stat_tiles, norm = x_tiles, (xn, x_tiles, 4 * b + 2)
                if h == H - 1 and not isinstance(b, int):
                    ended = xn, x_tiles, s["xn_ready"]
                if stat_tiles and h != FFN_HEAD:
                    norm_stats(stat_tiles, (0, 1))
                if ended and h != FFN_HEAD + 1:
                    normalise(ended[0], ended[1], (2, 3)).then_inc(ended[2], 1)
                if h < H - 1:
                    lookahead(g0 + 2)
                invert_sum(1, g0)
                max_row(2, h)
                if routing == 2:
                    add_router_bias(finishing, b_u)
                max_row(3, h)
                if ended and h == FFN_HEAD + 1:
                    normalise(ended[0], ended[1], (2, 3)).then_inc(ended[2], 1)
                if routing == 2:
                    max_logit()
                if stat_tiles:
                    norm_stats(stat_tiles, range(4) if h == FFN_HEAD else (2, 3))
                invert_sum(2, g0)
                if routing == 2:
                    shift_logits()
                invert_sum(3, g0)
                if stat_tiles:
                    norm_aggregate()
                if finishing is not None and h == 1:
                    x1n_low(finishing, b_u)
                if h < H - 1:
                    silu(g0 + 2, h + 1)
                    q_low(g0 + 2)
                elif not isinstance(b, int):
                    x_low(b + 2)
                if routing == 2:
                    sum_gates(finishing)
                if routing == 3:
                    rank_ties(finishing)
                p_low(h, 0, 3 * g0 + 1)
                if routing == 2:
                    invert_gate_sum()
                if routing == 3:
                    rank_all()
                p_low(h, 1, 3 * g0 + 2)
                if routing == 2:
                    scale_gates()
                if routing == 3:
                    keep_first_ties()
                if norm:
                    dve.wait_ge(s["rstd_ready"], norm[2])
                    normalise(norm[0], norm[1], (0, 1))
                if h == H - 1 or (h == FFN_HEAD - 1 and not isinstance(b, int)):
                    p_low(h, 2, 3 * g0 + 3)
                if routing == 3:
                    choose_experts()

            def x1n_low(b, src):
                dve.wait_ge(s["yhi_made"], b + 1)
                low_part(y_lo[:, :], src[:, :], y_hi[:, :]).then_inc(s["ylo_made"], 1)

            wide, pairs = [P, NT, E], [P, NT, E, E]

            def step(ins):
                ins.then_inc(s["route_step"], 1)
                dve.reg_add(step_count, step_count, 1)

            def wait_step():
                dve.wait_ge(s["consts_made"], 8)
                dve.wait_ge(s["route_step"], step_count)

            def add_router_bias(b, src):
                dve.wait_ge(s["stored"], 16)
                dve.wait_ge(s["logits_made"], b + 1)
                raw = src[:, 0:NT * 16].rearrange("p (t e) -> p t e", t=NT)[:, :, 0:E]
                v.tensor_tensor(logits[:, :, :], raw, rb[:, :].unsqueeze(1).to_broadcast(wide), ALU.add)\
                    .then_inc(s["logits_moved"], 1)
                dve.reg_add(logit_count, logit_count, 1)

            def max_logit():
                dve.wait_ge(s["consts_made"], 8)
                dve.wait_ge(s["logits_moved"], logit_count)
                step(v.tensor_reduce(top[:, :], logits[:, :, :], AX.X, ALU.max))

            def shift_logits():
                wait_step()
                v.tensor_tensor(logits[:, :, :], logits[:, :, :], top[:, :].unsqueeze(2).to_broadcast(wide), ALU.subtract)\
                    .then_inc(s["logits_shifted"], 1)

            def sum_gates(b):
                dve.wait_ge(s["gates_exped"], b + 1)
                step(v.tensor_reduce(route_sum[:, :], gates[:, :, :], AX.X, ALU.add))

            def invert_gate_sum():
                wait_step()
                step(v.reciprocal(route_inv[:, :], route_sum[:, :]))

            def scale_gates():
                wait_step()
                step(v.tensor_tensor(gates[:, :, :], gates[:, :, :], route_inv[:, :].unsqueeze(2).to_broadcast(wide), ALU.mult))

            def largest_gates():
                wait_step()
                for t in range(NT):
                    last = v.max(top8[:, t, :], gates[:, t, :])
                step(last)

            def compare_gates():
                kth = top8[:, :, TOPK - 1:TOPK].to_broadcast(wide)
                wait_step()
                v.tensor_tensor(above[:, :, :], gates[:, :, :], kth, ALU.is_gt)
                step(v.tensor_tensor(ties[:, :, :], gates[:, :, :], kth, ALU.is_equal))

            def count_above():
                wait_step()
                v.tensor_reduce(n_above[:, :], above[:, :, :], AX.X, ALU.add).then_inc(s["ties_ready"], 1)

            def rank_ties(b):
                dve.wait_ge(s["ties_masked"], b + 1)
                step(v.tensor_reduce(rank[:, :, :], tied[:, :, :, :], AX.X, ALU.add))

            def rank_all():
                wait_step()
                step(v.tensor_tensor(rank[:, :, :], rank[:, :, :], n_above[:, :].unsqueeze(2).to_broadcast(wide), ALU.add))

            def keep_first_ties():
                wait_step()
                step(v.scalar_tensor_tensor(ties[:, :, :], rank[:, :, :], float(TOPK), ties[:, :, :], ALU.is_lt, ALU.mult))

            def choose_experts():
                wait_step()
                step(v.tensor_tensor(ties[:, :, :], ties[:, :, :], above[:, :, :], ALU.add))
                wait_step()
                v.tensor_tensor(cw[:, :, 0:E], ties[:, :, :], gates[:, :, :], ALU.mult).then_inc(s["cw_ready"], 1)

            def experts(b):
                dve.wait_ge(s["cw_ready"], b + 1)
                for e in range(EA):
                    if e == BIAS_BEFORE:
                        dve.wait_ge(s["ye_added"], EA * b + e)
                        dve.wait_ge(s["bias_made"], b + 1)
                        v.tensor_tensor(ffn[:, :, :], b_cw[:, :].rearrange("p (t n) -> p t n", t=NT), ffn[:, :, :], ALU.add)\
                            .then_inc(s["bias_added"], 1)
                        dve.wait_ge(s["bias_added"], b + 1)
                    elif e:
                        dve.wait_ge(s["ye_added"], EA * b + e)
                    if e == EA - 1 and not isinstance(b, int):
                        dve.wait_ge(s["silu_masked"], H * b + H + FFN_HEAD + 1)
                        max_row(0, FFN_HEAD)
                    dve.wait_ge(s["ye_made"], EA * b + e + 1)
                    for t in range(NT):
                        made, weight = YE_BANK[e % 4][:, t * P:(t + 1) * P], cw[:, t, e:e + 1]
                        if e == 0:
                            last = v.tensor_scalar(ffn[:, t, :], made, weight, None, ALU.mult)
                        else:
                            last = v.scalar_tensor_tensor(ffn[:, t, :], made, weight, ffn[:, t, :], ALU.mult, ALU.add)
                    last.then_inc(s["ye_added"], 1)

            def move_attention(b):
                dve.wait_ge(s["att_made"], b + 1)
                v.tensor_copy(att_t[:, :], b_att[:, :]).then_inc(s["att_moved"], 1)

            def norm_attention(b, n):
                dve.wait_ge(s["rstd_ready"], n)
                normalise(normed, att_tiles).then_inc(s["normed_made"], 1)

            for k in (1, 3):
                move_values(k, k + 1)
            q_low(1)
            lookahead(1)
            for k in range(8, 11):
                value_low(k, 0)
            silu(1, 0)
            for k in range(11, 13):
                value_low(k, 0)
            for h in range(LOOP_HEAD):
                head(0, h)

            with dve.Fori(0, B - 1) as b:
                for h in range(LOOP_HEAD, H):
                    head(b, h)
                v0 = 16 * b + 17
                move_values(1, v0 + 1)
                move_values(3, v0 + 3)
                move_attention(b)
                q_low(H * b + H + 1)
                dve.wait_ge(s["atok_made"], b + 1)
                norm_stats(att_tiles)
                lookahead(H * b + H + 1)
                norm_aggregate()
                value_low(8, b + 1)
                norm_attention(b, 4 * b + 3)
                silu(H * b + H + 1, 0)
                for k in range(9, 13):
                    value_low(k, b + 1)
                for h in range(FFN_HEAD):
                    head(b + 1, h, finishing=b)
                experts(b)
                for h in range(FFN_HEAD, LOOP_HEAD):
                    head(b + 1, h, finished=b)
            for h in range(LOOP_HEAD, H):
                head(B - 1, h)
            last_b = B - 1
            move_attention(last_b)
            dve.wait_ge(s["atok_made"], last_b + 1)
            norm_stats(att_tiles)
            norm_aggregate()
            norm_attention(last_b, 4 * last_b + 2)
            dve.wait_ge(s["res_loaded"], 16 * last_b + 16)
            dve.wait_ge(s["normed_made"], 2 * last_b + 1)
            v.tensor_tensor(x1[:, :, :], normed[:, :, :], x_res[:, :, :], ALU.add).then_inc(s["x1_ready"], 1)
            dve.wait_ge(s["x1_ready"], last_b + 1)
            norm_stats(x1_tiles)
            norm_aggregate()
            dve.wait_ge(s["rstd_ready"], 4 * last_b + 3)
            normalise(x1n, x1_tiles).then_inc(s["x1n_ready"], 1)
            x1n_low(last_b, b_u)
            add_router_bias(last_b, b_att)
            max_logit()
            shift_logits()
            sum_gates(last_b)
            invert_gate_sum()
            scale_gates()
            largest_gates()
            compare_gates()
            count_above()
            rank_ties(last_b)
            rank_all()
            keep_first_ties()
            choose_experts()
            experts(last_b)
            dve.wait_ge(s["ye_added"], EA * B)
            norm_stats(ffn_tiles)
            norm_aggregate()
            dve.wait_ge(s["rstd_ready"], 4 * last_b + 4)
            normalise(normed, ffn_tiles).then_inc(s["normed_made"], 1)
            dve.wait_ge(s["stored"], 16 * last_b + 16)
            dve.wait_ge(s["normed_made"], 2 * last_b + 2)
            v.tensor_tensor(result[:, :, :], normed[:, :, :], x1[:, :, :], ALU.add).then_inc(s["result_ready"], 1)


_INS = ["x", "w_qkv", "w_out", "router_W", "router_b", "sW1", "sb1", "sW2", "sb2", "eW1", "eb1", "eW2", "eb2"]


def kernel(**inputs):
    import numpy as np
    import concourse.bacc as bacc
    from concourse.bass_utils import run_bass_kernel_spmd

    nc = bacc.Bacc("TRN2", target_bir_lowering=False, num_devices=1)
    arrays, args = {}, []
    for n in _INS:
        a = np.ascontiguousarray(inputs[("L0_attn_" if n in _INS[:3] else "L0_ffn_") + n])
        arrays[f"in_{n}"] = a
        args.append(nc.dram_tensor(f"in_{n}", a.shape, F32, kind="ExternalInput").ap())
    args.append(nc.dram_tensor("out", (B, S, D), F32, kind="ExternalOutput").ap())
    castle_moe(nc, *args)
    return run_bass_kernel_spmd(nc, [arrays], core_ids=[0]).results[0]["out"]
```
